# Optimizing a Trainium2 kernel written in Bass

```python
import numpy as np
import jax
import jax.numpy as jnp

def _softmax(x, axis=-1):
    return jax.nn.softmax(x, axis=axis)

def _gelu(x):
    return jax.nn.gelu(x, approximate=True)

def _silu(x):
    return jax.nn.silu(x)

def _sigmoid(x):
    return jax.nn.sigmoid(x)

def _layernorm(x, axis=-1, eps=1e-05):
    m = jnp.mean(x, axis=axis, keepdims=True)
    v = jnp.var(x, axis=axis, keepdims=True)
    return (x - m) / jnp.sqrt(v + eps)

def _scatter_add(tgt, idx, src, axis=0):
    return tgt.at[idx].add(src)

def _segment_sum(src, seg, n):
    return jax.ops.segment_sum(src, seg, n)
kernel_name = 'mk_audio_tower_d1_tok_aud1d768_r4_a12a73'

def setup_inputs(seed: int=0):
    np.random.seed(seed)
    _w = jnp.asarray

    def _rec_inputs():
        import jax
        import jax.numpy as jnp
        _rk = jax.random.key(seed)
        x = -6.41493e-05 + 1.00002 * jax.random.normal(jax.random.fold_in(_rk, 1), (64, 4000), jnp.float32)
        return x
    x = _rec_inputs()

    def _L0_tok_setup():
        import jax, jax.numpy as jnp
        import numpy as np
        import math
        SR = 4000
        FRAME_LEN = 100
        FRAME_STEP = 160
        N_FILTERS = 40
        N_MFCC = 13
        EMBED = 192
        BATCH = 64
        AUDIO_LEN = 40000
        N_FFT_BINS = FRAME_LEN // 2 + 1

        def _mel_filterbank():
            low_mel = 2595.0 * math.log10(1.0 + 0.0 / 700.0)
            high_mel = 2595.0 * math.log10(1.0 + SR // 2 / 700.0)
            mel_points = np.linspace(low_mel, high_mel, N_FILTERS + 2)
            hz_points = 700.0 * (10.0 ** (mel_points / 2595.0) - 1.0)
            bin_points = np.floor((FRAME_LEN + 1) * hz_points / SR)
            filt = np.zeros((N_FILTERS, N_FFT_BINS), dtype=np.float32)
            for i in range(1, N_FILTERS + 1):
                l, c, r = (bin_points[i - 1], bin_points[i], bin_points[i + 1])
                for j in range(int(l), int(c)):
                    filt[i - 1, j] = (j - l) / (c - l)
                for j in range(int(c), int(r)):
                    filt[i - 1, j] = (r - j) / (r - c)
            return jnp.asarray(filt)

        def _dct_matrix():
            k = np.arange(N_MFCC)[:, None]
            j = np.arange(N_FILTERS)[None, :]
            m = np.cos(np.pi * k * (2 * j + 1) / (2 * N_FILTERS)) * math.sqrt(2.0 / N_FILTERS)
            return jnp.asarray(m.astype(np.float32))
        key = jax.random.key(seed)
        kx, kw = jax.random.split(key)
        x = jax.random.normal(kx, (BATCH, AUDIO_LEN), dtype=jnp.float32)
        bound = 1.0 / math.sqrt(N_MFCC)
        w_proj = jax.random.uniform(kw, (N_MFCC, EMBED), minval=-bound, maxval=bound, dtype=jnp.float32)
        b_proj = jnp.zeros((EMBED,), dtype=jnp.float32)
        return {'x': x, 'mel_filters': _mel_filterbank(), 'dct': _dct_matrix(), 'w_proj': w_proj, 'b_proj': b_proj}
    _L0_tok_all = _L0_tok_setup()
    _L0_tok_in = {k: v for k, v in _L0_tok_all.items() if k in ('mel_filters', 'dct', 'w_proj', 'b_proj')}
    del _L0_tok_all

    def _L0_attn_setup():
        import jax, jax.numpy as jnp
        import numpy as np
        D = 192
        ORDER = 2
        K = 3
        MAXLEN = 512

        def _fft_conv(h, x, Bp):
            L = x.shape[-1]
            n = 2 * L
            h_f = jnp.fft.rfft(h, n=n, norm='forward')
            x_f = jnp.fft.rfft(x, n=n)
            y = jnp.fft.irfft(h_f * x_f, n=n, norm='forward')[..., :L]
            return y + x * Bp
        key = jax.random.key(seed)
        ks = jax.random.split(key, 8)
        Bsz, L = (4, 512)
        C = D * (ORDER + 1)
        u = jax.random.normal(ks[0], (Bsz, L, D), jnp.float32)
        W_lin = jax.random.normal(ks[1], (C, D), jnp.float32) / np.float32(np.sqrt(D))
        b_lin = jnp.zeros((C,), jnp.float32)
        conv_w = jax.random.normal(ks[2], (C, 1, K), jnp.float32) / np.float32(np.sqrt(K))
        conv_b = jnp.zeros((C,), jnp.float32)
        W_out = jax.random.normal(ks[3], (D, D), jnp.float32) / np.float32(np.sqrt(D))
        b_out = jnp.zeros((D,), jnp.float32)
        h_param = jax.random.normal(ks[4], (ORDER, D, MAXLEN), jnp.float32)
        win_b = jnp.zeros((1, D, 1), jnp.float32)
        min_decay = np.log(0.01) / 1.5
        max_decay = np.log(0.01) / 0.3
        alphas = jnp.linspace(min_decay, max_decay, D, dtype=jnp.float32)[None, :, None]
        Bmat = jax.random.normal(ks[5], (ORDER, 1, D, 1), jnp.float32)
        return dict(u=u, W_lin=W_lin, b_lin=b_lin, conv_w=conv_w, conv_b=conv_b, W_out=W_out, b_out=b_out, h_param=h_param, win_b=win_b, alphas=alphas, Bmat=Bmat)
    _L0_attn_all = _L0_attn_setup()
    _L0_attn_in = {k: v for k, v in _L0_attn_all.items() if k in ('W_lin', 'b_lin', 'conv_w', 'conv_b', 'W_out', 'b_out', 'h_param', 'win_b', 'alphas', 'Bmat')}
    del _L0_attn_all

    def _L0_ffn_setup():
        import jax, jax.numpy as jnp
        import numpy as np
        import math
        N_HEAD = 12
        N_EXP = 8
        TOP_K = 2
        EVAL_CAPACITY = 1.0
        MIN_CAPACITY = 4
        EPS = 1e-05

        def layer_norm(x, w):
            mu = jnp.mean(x, axis=-1, keepdims=True)
            var = jnp.var(x, axis=-1, keepdims=True)
            return (x - mu) / jnp.sqrt(var + EPS) * w

        def attention(x, c_attn_w, c_proj_w):
            B, T, C = x.shape
            H, D = (N_HEAD, C // N_HEAD)
            qkv = x @ c_attn_w.T
            q, k, v = jnp.split(qkv, 3, axis=-1)
            q = q.reshape(B, T, H, D).transpose(0, 2, 1, 3)
            k = k.reshape(B, T, H, D).transpose(0, 2, 1, 3)
            v = v.reshape(B, T, H, D).transpose(0, 2, 1, 3)
            scores = jnp.einsum('bhqd,bhkd->bhqk', q, k) * (1.0 / math.sqrt(D))
            causal = jnp.tril(jnp.ones((T, T), dtype=bool))
            scores = jnp.where(causal, scores, -jnp.inf)
            att = jax.nn.softmax(scores, axis=-1)
            y = jnp.einsum('bhqk,bhkd->bhqd', att, v)
            y = y.transpose(0, 2, 1, 3).reshape(B, T, C)
            return y @ c_proj_w.T

        def get_capacity(num_tokens):
            cap = int(math.floor(TOP_K * EVAL_CAPACITY * num_tokens / N_EXP))
            cap += cap % 2
            return max(cap, MIN_CAPACITY)

        def moe(x_flat, w_g, c_fc, c_proj_e):
            n_tok, C = x_flat.shape
            logits = x_flat @ w_g.T
            top_vals, top_idx = jax.lax.top_k(logits, TOP_K)
            rows = jnp.arange(n_tok)[:, None]
            masked = jnp.full_like(logits, -jnp.inf).at[rows, top_idx].set(top_vals)
            probs = jax.nn.softmax(masked, axis=-1)
            cap = get_capacity(n_tok)
            flat_e = top_idx.reshape(-1)
            onehot = jax.nn.one_hot(flat_e, N_EXP, dtype=jnp.int32)
            pos = jnp.cumsum(onehot, axis=0) - onehot
            slot = jnp.take_along_axis(pos, flat_e[:, None], axis=1)[:, 0]
            valid = slot < cap
            tok = jnp.repeat(jnp.arange(n_tok), TOP_K)
            slot_c = jnp.where(valid, slot, cap)
            sec = jnp.zeros((n_tok, N_EXP, cap + 1), dtype=x_flat.dtype)
            sec = sec.at[tok, flat_e, slot_c].set(1.0)[:, :, :cap]
            w_tok = probs[tok, flat_e]
            cb = jnp.zeros((n_tok, N_EXP, cap + 1), dtype=x_flat.dtype)
            cb = cb.at[tok, flat_e, slot_c].set(w_tok)[:, :, :cap]
            dispatched = jnp.einsum('tec,td->ecd', sec, x_flat)
            h = jax.nn.gelu(jnp.einsum('ecd,edh->ech', dispatched, c_fc), approximate=False)
            out = jnp.einsum('ech,ehd->ecd', h, c_proj_e)
            return jnp.einsum('tec,ecd->td', cb, out)
        key = jax.random.key(seed)
        ks = jax.random.split(key, 7)
        B, T, C = (2, 512, 192)
        std = 0.02
        return {'x': jax.random.normal(ks[0], (B, T, C), dtype=jnp.float32), 'ln1_w': jnp.ones((C,), dtype=jnp.float32), 'ln2_w': jnp.ones((C,), dtype=jnp.float32), 'c_attn_w': jax.random.normal(ks[1], (3 * C, C), dtype=jnp.float32) * std, 'c_proj_w': jax.random.normal(ks[2], (C, C), dtype=jnp.float32) * std, 'w_g': jax.random.normal(ks[3], (N_EXP, C), dtype=jnp.float32) * std, 'c_fc': jax.random.normal(ks[4], (N_EXP, C, 4 * C), dtype=jnp.float32) * std, 'c_proj_e': jax.random.normal(ks[5], (N_EXP, 4 * C, C), dtype=jnp.float32) * std}
    _L0_ffn_all = _L0_ffn_setup()
    _L0_ffn_in = {k: v for k, v in _L0_ffn_all.items() if k in ('ln1_w', 'ln2_w', 'c_attn_w', 'c_proj_w', 'w_g', 'c_fc', 'c_proj_e')}
    del _L0_ffn_all
    return {'x': x, 'L0_tok_mel_filters': _L0_tok_in['mel_filters'], 'L0_tok_dct': _L0_tok_in['dct'], 'L0_tok_w_proj': _L0_tok_in['w_proj'], 'L0_tok_b_proj': _L0_tok_in['b_proj'], 'L0_attn_W_lin': _L0_attn_in['W_lin'], 'L0_attn_b_lin': _L0_attn_in['b_lin'], 'L0_attn_conv_w': _L0_attn_in['conv_w'], 'L0_attn_conv_b': _L0_attn_in['conv_b'], 'L0_attn_W_out': _L0_attn_in['W_out'], 'L0_attn_b_out': _L0_attn_in['b_out'], 'L0_attn_h_param': _L0_attn_in['h_param'], 'L0_attn_win_b': _L0_attn_in['win_b'], 'L0_attn_alphas': _L0_attn_in['alphas'], 'L0_attn_Bmat': _L0_attn_in['Bmat'], 'L0_ffn_ln1_w': _L0_ffn_in['ln1_w'], 'L0_ffn_ln2_w': _L0_ffn_in['ln2_w'], 'L0_ffn_c_attn_w': _L0_ffn_in['c_attn_w'], 'L0_ffn_c_proj_w': _L0_ffn_in['c_proj_w'], 'L0_ffn_w_g': _L0_ffn_in['w_g'], 'L0_ffn_c_fc': _L0_ffn_in['c_fc'], 'L0_ffn_c_proj_e': _L0_ffn_in['c_proj_e']}

def reference(x, L0_tok_mel_filters, L0_tok_dct, L0_tok_w_proj, L0_tok_b_proj, L0_attn_W_lin, L0_attn_b_lin, L0_attn_conv_w, L0_attn_conv_b, L0_attn_W_out, L0_attn_b_out, L0_attn_h_param, L0_attn_win_b, L0_attn_alphas, L0_attn_Bmat, L0_ffn_ln1_w, L0_ffn_ln2_w, L0_ffn_c_attn_w, L0_ffn_c_proj_w, L0_ffn_w_g, L0_ffn_c_fc, L0_ffn_c_proj_e):
    import jax
    import jax.numpy as jnp

    def _L0_tok_ref(x, mel_filters, dct, w_proj, b_proj):
        import jax, jax.numpy as jnp
        import numpy as np
        import math
        SR = 4000
        FRAME_LEN = 100
        FRAME_STEP = 160
        N_FILTERS = 40
        N_MFCC = 13
        EMBED = 192
        BATCH = 64
        AUDIO_LEN = 40000
        N_FFT_BINS = FRAME_LEN // 2 + 1

        def _mel_filterbank():
            low_mel = 2595.0 * math.log10(1.0 + 0.0 / 700.0)
            high_mel = 2595.0 * math.log10(1.0 + SR // 2 / 700.0)
            mel_points = np.linspace(low_mel, high_mel, N_FILTERS + 2)
            hz_points = 700.0 * (10.0 ** (mel_points / 2595.0) - 1.0)
            bin_points = np.floor((FRAME_LEN + 1) * hz_points / SR)
            filt = np.zeros((N_FILTERS, N_FFT_BINS), dtype=np.float32)
            for i in range(1, N_FILTERS + 1):
                l, c, r = (bin_points[i - 1], bin_points[i], bin_points[i + 1])
                for j in range(int(l), int(c)):
                    filt[i - 1, j] = (j - l) / (c - l)
                for j in range(int(c), int(r)):
                    filt[i - 1, j] = (r - j) / (r - c)
            return jnp.asarray(filt)

        def _dct_matrix():
            k = np.arange(N_MFCC)[:, None]
            j = np.arange(N_FILTERS)[None, :]
            m = np.cos(np.pi * k * (2 * j + 1) / (2 * N_FILTERS)) * math.sqrt(2.0 / N_FILTERS)
            return jnp.asarray(m.astype(np.float32))
        B, T = x.shape
        n_frames = 1 + (T - FRAME_LEN) // FRAME_STEP
        idx = jnp.arange(n_frames)[:, None] * FRAME_STEP + jnp.arange(FRAME_LEN)[None, :]
        frames = x[:, idx]
        window = 0.54 - 0.46 * jnp.cos(2.0 * jnp.pi * jnp.arange(FRAME_LEN, dtype=jnp.float32) / (FRAME_LEN - 1))
        windowed = frames * window
        fft = jnp.fft.rfft(windowed, axis=-1)
        power = fft.real ** 2 + fft.imag ** 2
        mel_energies = jnp.einsum('bnf,mf->bnm', power, mel_filters)
        log_energies = jnp.log(mel_energies + 1e-06)
        mfcc = jnp.einsum('bnm,km->bnk', log_energies, dct)
        out = mfcc @ w_proj + b_proj
        return out

    def _L0_attn_ref(u, W_lin, b_lin, conv_w, conv_b, W_out, b_out, h_param, win_b, alphas, Bmat):
        import jax, jax.numpy as jnp
        import numpy as np
        D = 192
        ORDER = 2
        K = 3
        MAXLEN = 512

        def _fft_conv(h, x, Bp):
            L = x.shape[-1]
            n = 2 * L
            h_f = jnp.fft.rfft(h, n=n, norm='forward')
            x_f = jnp.fft.rfft(x, n=n)
            y = jnp.fft.irfft(h_f * x_f, n=n, norm='forward')[..., :L]
            return y + x * Bp
        Bsz, L, d = u.shape
        z = (u @ W_lin.T + b_lin).transpose(0, 2, 1)
        z = jax.lax.conv_general_dilated(z, conv_w, window_strides=(1,), padding=[(K - 1, K - 1)], feature_group_count=z.shape[1], dimension_numbers=('NCH', 'OIH', 'NCH'))[..., :L] + conv_b[None, :, None]
        xs = [z[:, i * d:(i + 1) * d] for i in range(ORDER)]
        v = z[:, ORDER * d:] + u.transpose(0, 2, 1)
        t = jnp.linspace(0.0, 1.0, MAXLEN, dtype=u.dtype)[None, None, :L]
        h = h_param[:, :, :L] * (jnp.exp(alphas * t) + win_b)
        h = h / jnp.sum(jnp.abs(h), axis=-2, keepdims=True)
        for i in range(ORDER):
            v = v + jax.nn.softmax(xs[i], axis=1) * _fft_conv(h[i][None], v, Bmat[i])
        v = v.transpose(0, 2, 1)
        return v + v @ W_out.T + b_out

    def _L0_ffn_ref(x, ln1_w, ln2_w, c_attn_w, c_proj_w, w_g, c_fc, c_proj_e):
        import jax, jax.numpy as jnp
        import numpy as np
        import math
        N_HEAD = 12
        N_EXP = 8
        TOP_K = 2
        EVAL_CAPACITY = 1.0
        MIN_CAPACITY = 4
        EPS = 1e-05

        def layer_norm(x, w):
            mu = jnp.mean(x, axis=-1, keepdims=True)
            var = jnp.var(x, axis=-1, keepdims=True)
            return (x - mu) / jnp.sqrt(var + EPS) * w

        def attention(x, c_attn_w, c_proj_w):
            B, T, C = x.shape
            H, D = (N_HEAD, C // N_HEAD)
            qkv = x @ c_attn_w.T
            q, k, v = jnp.split(qkv, 3, axis=-1)
            q = q.reshape(B, T, H, D).transpose(0, 2, 1, 3)
            k = k.reshape(B, T, H, D).transpose(0, 2, 1, 3)
            v = v.reshape(B, T, H, D).transpose(0, 2, 1, 3)
            scores = jnp.einsum('bhqd,bhkd->bhqk', q, k) * (1.0 / math.sqrt(D))
            causal = jnp.tril(jnp.ones((T, T), dtype=bool))
            scores = jnp.where(causal, scores, -jnp.inf)
            att = jax.nn.softmax(scores, axis=-1)
            y = jnp.einsum('bhqk,bhkd->bhqd', att, v)
            y = y.transpose(0, 2, 1, 3).reshape(B, T, C)
            return y @ c_proj_w.T

        def get_capacity(num_tokens):
            cap = int(math.floor(TOP_K * EVAL_CAPACITY * num_tokens / N_EXP))
            cap += cap % 2
            return max(cap, MIN_CAPACITY)

        def moe(x_flat, w_g, c_fc, c_proj_e):
            n_tok, C = x_flat.shape
            logits = x_flat @ w_g.T
            top_vals, top_idx = jax.lax.top_k(logits, TOP_K)
            rows = jnp.arange(n_tok)[:, None]
            masked = jnp.full_like(logits, -jnp.inf).at[rows, top_idx].set(top_vals)
            probs = jax.nn.softmax(masked, axis=-1)
            cap = get_capacity(n_tok)
            flat_e = top_idx.reshape(-1)
            onehot = jax.nn.one_hot(flat_e, N_EXP, dtype=jnp.int32)
            pos = jnp.cumsum(onehot, axis=0) - onehot
            slot = jnp.take_along_axis(pos, flat_e[:, None], axis=1)[:, 0]
            valid = slot < cap
            tok = jnp.repeat(jnp.arange(n_tok), TOP_K)
            slot_c = jnp.where(valid, slot, cap)
            sec = jnp.zeros((n_tok, N_EXP, cap + 1), dtype=x_flat.dtype)
            sec = sec.at[tok, flat_e, slot_c].set(1.0)[:, :, :cap]
            w_tok = probs[tok, flat_e]
            cb = jnp.zeros((n_tok, N_EXP, cap + 1), dtype=x_flat.dtype)
            cb = cb.at[tok, flat_e, slot_c].set(w_tok)[:, :, :cap]
            dispatched = jnp.einsum('tec,td->ecd', sec, x_flat)
            h = jax.nn.gelu(jnp.einsum('ecd,edh->ech', dispatched, c_fc), approximate=False)
            out = jnp.einsum('ech,ehd->ecd', h, c_proj_e)
            return jnp.einsum('tec,ecd->td', cb, out)
        x = x + attention(layer_norm(x, ln1_w), c_attn_w, c_proj_w)
        B, T, C = x.shape
        x_ln = layer_norm(x, ln2_w)
        moe_out = moe(x_ln.reshape(B * T, C), w_g, c_fc, c_proj_e)
        return x + moe_out.reshape(B, T, C)
    h = _L0_tok_ref(x, L0_tok_mel_filters, L0_tok_dct, L0_tok_w_proj, L0_tok_b_proj)
    h = h + _L0_attn_ref(_layernorm(h, axis=-1), L0_attn_W_lin, L0_attn_b_lin, L0_attn_conv_w, L0_attn_conv_b, L0_attn_W_out, L0_attn_b_out, L0_attn_h_param, L0_attn_win_b, L0_attn_alphas, L0_attn_Bmat)
    h = h + _L0_ffn_ref(_layernorm(h, axis=-1), L0_ffn_ln1_w, L0_ffn_ln2_w, L0_ffn_c_attn_w, L0_ffn_c_proj_w, L0_ffn_w_g, L0_ffn_c_fc, L0_ffn_c_proj_e)
    return h

_drawn_inputs = setup_inputs


def setup_inputs(seed=0):
    import zlib

    import numpy as np

    out = dict(_drawn_inputs(seed))
    spreads = {'L0_tok_b_proj': (0.0, 0.314),
     'L0_attn_b_lin': (0.0, 0.279),
     'L0_attn_conv_b': (0.0, 0.28),
     'L0_attn_b_out': (0.0, 0.426),
     'L0_attn_win_b': (0.0, 0.8),
     'L0_ffn_ln1_w': (1.0, 0.6),
     'L0_ffn_ln2_w': (1.0, 0.6)}
    factors = {'L0_attn_h_param': 8.0,
     'L0_attn_alphas': 8.0,
     'L0_attn_Bmat': 3.984,
     'L0_ffn_c_attn_w': 4.187,
     'L0_ffn_c_proj_w': 4.183,
     'L0_ffn_w_g': 8.0,
     'L0_ffn_c_fc': 8.0,
     'L0_ffn_c_proj_e': 8.0}
    for name, (base, spread) in spreads.items():
        noise = np.random.default_rng([zlib.crc32(name.encode()), seed]).standard_normal(out[name].shape)
        drawn = base * np.exp(spread * noise) if base else spread * noise
        out[name] = jnp.asarray(drawn.astype(out[name].dtype))
    for name, factor in factors.items():
        out[name] = (out[name] * factor).astype(out[name].dtype)
    return out
```

```python
from contextlib import ExitStack

import concourse.bass as bass
from concourse import mybir

ALU = mybir.AluOpType
ACT = mybir.ActivationFunctionType
AX = mybir.AxisListType
F32 = mybir.dt.float32
BF16 = mybir.dt.bfloat16
U32 = mybir.dt.uint32

B, T, D = 64, 25, 192
G = 5
R = G * T
NT = -(-B // G)
LAST = (B - (NT - 1) * G) * T
TOKENS = B * T
FRAME, HOP, BINS, MELS, MFCC = 100, 160, 51, 40, 13
DC = D // 2
KW = 3
ZC = [128, 128, 128, 128, 64]
NF = 2 * T - 1
FR = 3 * (NF // 2) + 1
FC = -(-G * FR // 3)
HEADS, HD = 12, 16
HG = 4
NG = HEADS // HG
GD = HG * HD
E, TOPK, FF = 8, 2, 4 * D
CAP = TOPK * TOKENS // E
SQ = 4
SR = CAP // SQ
MC = FF // 128
ROW = D + 4
NOWHERE = float(1 << 22)
EPS = 1e-5
SCALE = HD ** -0.5
MASKED = -1e30


def constants():
    import numpy as np
    c = {}
    n = np.arange(FRAME)
    window = 0.54 - 0.46 * np.cos(2.0 * np.pi * n / (FRAME - 1))
    ang = 2.0 * np.pi * np.outer(n, np.arange(BINS)) / FRAME
    c["dft"] = np.concatenate([np.cos(ang), -np.sin(ang)], 1) * window[:, None]
    t = np.arange(T)
    fwd, coef, inv = [np.ones(T)], [np.ones(T)], [np.ones(T) / NF]
    for f in range(1, NF // 2 + 1):
        co, si = np.cos(2 * np.pi * f * t / NF), np.sin(2 * np.pi * f * t / NF)
        fwd += [co - si, co, -si]
        coef += [co, -si - co, co - si]
        inv += [2 * (co - si) / NF, -2 * si / NF, -2 * co / NF]
    fwd, coef, inv = np.array(fwd), np.array(coef), np.array(inv)
    A = np.zeros((R, 3 * FC)); H = np.zeros((T, 3 * FC)); V = np.zeros((3 * FC, R))
    for b in range(G):
        r, k = slice(b * T, b * T + T), slice(b * FR, b * FR + FR)
        A[r, k] = fwd.T
        H[:, k] = coef.T
        V[k, r] = inv
    c["fwd"], c["coef"] = A, H
    c["inv"] = V.reshape(3, FC, R).transpose(1, 0, 2).reshape(FC, 3 * R)
    c["time"] = np.tile(np.linspace(0.0, 1.0, 512, dtype=np.float32)[:T], (DC, 1))
    c["ident"] = np.eye(128)
    head_of_row = (np.arange(128) % GD) // HD
    c["kmask"] = (head_of_row[:, None] == np.repeat(np.arange(HG), T)[None]) * 1.0
    sel = np.zeros((R, G, HG * T))
    for b in range(G):
        for h in range(HG):
            for k in range(T):
                sel[b * T + k, b, h * T + k] = 1.0
    c["sel"] = sel.reshape(R, -1)
    vh = (np.arange(D) % GD) // HD
    c["vmask"] = (np.repeat(np.arange(HG), T)[:, None] == vh[None]) * 1.0
    q = np.arange(R) % T
    c["causal"] = np.where(np.tile(np.arange(T), HG)[None] > q[:, None], MASKED, 0.0)
    c["before"] = (np.arange(R)[:, None] < np.arange(R)[None]) * 1.0
    c["expert"] = np.tile(np.arange(E), (128, 1))
    c["token"] = np.arange(R)[:, None] + R * np.arange(NT)[None]
    return {k: np.ascontiguousarray(v, dtype=np.float32) for k, v in c.items()}


def tower(nc, a, out):
    with ExitStack() as ctx:
        def sb(name, shape, dt=F32):
            return ctx.enter_context(nc.sbuf_tensor(name, shape, dt))

        S = {}

        def sem(name):
            S[name] = ctx.enter_context(nc.semaphore("s_" + name))
            return S[name]

        slots = nc.dram_tensor("slots", [E * CAP, ROW], F32).ap()

        frames = sb("frames", [FRAME, NT * R])
        dft = sb("dft", [FRAME, 2 * BINS])
        melT = sb("melT", [2 * BINS, MELS])
        dct = sb("dct_s", [MFCC, MELS])
        wtok = sb("wtok", [MFCC, D])
        tokw = sb("tokw", [MELS + 1, D])
        wlin = sb("wlin", [DC + 1, 2, 3 * D])
        taps = sb("taps", [128, 5, KW])
        tapb = sb("tapb", [128, 5])
        fwd = sb("fwd", [R, 3, FC])
        coef = sb("coef", [T, 3, FC])
        inv = sb("inv", [FC, 3, R])
        hfil = sb("hfil", [DC, 2, 2, T])
        hdec = sb("hdec", [DC, 2, T])
        alph = sb("alph", [DC, 2])
        winb = sb("winb", [DC, 2])
        bmat = sb("bmat", [1, 2, D])
        hT = sb("hT", [T, 2, D])
        habs = sb("habs", [T, 2])
        hrec = sb("hrec", [T, 2])
        hcoef = sb("hcoef", [FC, 2, 3, D])
        times = sb("times", [DC, T])
        wout = sb("wout", [DC + 1, 2, D])
        ident = sb("ident", [128, 128])
        identb = sb("identb", [128, 128], BF16)
        ln1 = sb("ln1", [DC, 2])
        ln2 = sb("ln2", [DC, 2])
        wqkv = sb("wqkv", [DC, 2, 3 * D])
        wo = sb("wo", [128, 2, D])
        kmask = sb("kmask", [128, HG * T])
        sel = sb("sel", [R, G, HG * T])
        vmask = sb("vmask", [HG * T, D])
        causal = sb("causal", [R, HG * T])
        causalb = sb("causalb", [R, HG * T], BF16)
        before = sb("before", [R, R])
        beforeb = sb("beforeb", [R, R], BF16)
        onesb = sb("onesb", [R, R], BF16)
        expert = sb("expert", [128, E])
        token = sb("token", [R, NT])
        wgate = sb("wgate", [DC, 2, E])
        wfc = sb("wfc", [DC, E, 2, FF])
        wpr = sb("wpr", [128, E, MC, D])
        epsc = sb("epsc", [128, 2])
        fill = sb("fill", [SR, SQ, ROW])

        def two(name, shape, dt=F32):
            x = sb(name, [shape[0], 2] + shape[1:], dt)
            return [x[:, p] for p in range(2)]

        early = ExitStack()
        late = sb

        def sb(name, shape, dt=F32):
            return early.enter_context(nc.sbuf_tensor(name, shape, dt))


        sq = two("sq", [2 * BINS, R])
        logmel = two("logmel", [64, R])
        h0 = two("h0", [R, D])
        u = two("u", [R, D])
        uT = two("uT", [DC + 1, 2, R])
        z = two("z", [128, 5, G, T + KW - 1])
        y = two("y", [128, 5, R])
        early.close()
        sb = late
        hid = two("hid", [128, MC, CAP])
        ex = two("ex", [R, 2, D])
        nmax = two("nmax", [R, 2])
        ssum = two("ssum", [R, 2])
        rsum = two("rsum", [R, 2])
        v = two("v", [R, D])
        prod = sb("prod", [FC, 3, D])
        gate = sb("gate", [R, D])
        vT = two("vT", [DC + 1, 2, R])
        hv = sb("hv", [R, D])
        h1 = two("h1", [R, D])
        xp = two("xp", [R, D])
        an = two("an", [R, D])
        stat = sb("stat", [R, 3, 6])
        mv = sb("mv", [R, 3, 2])
        lnv = sb("lnv", [R, 4])
        rstd = sb("rstd", [R, 4])
        var2 = sb("var2", [R, 1])
        aT = two("aT", [DC, 2, R])
        qpad = sb("qpad", [128, 2, G, R])
        kx = sb("kx", [128, 2, G, HG * T])
        vt = sb("vt", [R, D])
        vx = sb("vx", [HG * T, G, D])
        smax = sb("smax", [R, HEADS])
        sc = sb("sc", [R, HEADS, T])
        es = sb("es", [R, HEADS, T])
        psm = sb("psm", [R, HEADS])
        prc = sb("prc", [R, HEADS])
        pn = sb("pn", [R, HEADS, T])
        pT = sb("pT", [HG * T, NG, R])
        yT = sb("yT", [128, 2, R])
        h2 = two("h2", [R, D])
        base = two("base", [R, D])
        xl = two("xl", [R, ROW])
        xlT = sb("xlT", [DC, 2, R])
        top = two("top", [R, 8])
        topi = two("topi", [R, 8], U32)
        ef = two("ef", [R, 2])
        diff = sb("diff", [R, 1])
        ed = sb("ed", [R, 1])
        den = sb("den", [R, 1])
        oh = sb("oh", [R, 2, E])
        chosen = two("chosen", [R, E], BF16)
        total = two("total", [R, E], BF16)
        junk = sb("junk", [R, 2, E])
        slot = sb("slot", [R, 2])
        over = sb("over", [R, 2])
        at = sb("at", [R, 2])
        atu = two("atu", [R, 2], U32)
        xe = two("xe", [SR, SQ, ROW])
        xeT = two("xeT", [DC, 2, CAP])
        ye = two("ye", [SR, SQ, D])
        first = sb("first", [SR, SQ])
        wa = sb("wa", [SR, SQ])
        wb = sb("wb", [SR, SQ])
        wt = two("wt", [SR, SQ])
        tok = two("tok", [SR, SQ], U32)

        PB = [ctx.enter_context(nc.psum_tensor(f"bank{i}", [128, 512], F32)) for i in range(8)]
        pspec, pmel, ptok = PB[0][0:2 * BINS, 0:R], PB[0][0:MELS, 0:R], PB[0][0:R, 0:D]
        puT = PB[0][0:DC, 0:2 * R].rearrange("p (c n) -> p c n", c=2)
        pz = PB[1][:, 0:4 * R].rearrange("p (c n) -> p c n", c=4)
        px = PB[1][0:R, 0:2 * D]
        pz4 = PB[2][0:64, 0:R]
        pv = PB[2][0:R, 0:D]
        pf01, pf2, py = PB[3][0:FC, 0:2 * D], PB[4][0:FC, 0:D], PB[4][0:R, 0:D]
        pvT = PB[3][0:DC, 0:2 * R].rearrange("p (c n) -> p c n", c=2)
        po = PB[4][0:R, 0:D]
        paT = PB[5][0:DC, 0:2 * R].rearrange("p (c n) -> p c n", c=2)
        pq = PB[5][:, 0:2 * R].rearrange("p (c n) -> p c n", c=2)
        pvv = PB[5][0:R, 256:256 + D]
        pk = PB[6][:, 0:2 * R].rearrange("p (c n) -> p c n", c=2)
        ps1 = PB[5][0:R, 0:HG * T].rearrange("p (h k) -> p h k", k=T)
        ps02 = PB[6][0:R, 0:2 * HG * T].rearrange("p (h k) -> p h k", k=T)
        ppT = PB[5][0:HG * T, 0:NG * R].rearrange("p (g n) -> p g n", g=NG)
        pvx = PB[7][0:HG * T, 0:2 * D].rearrange("p (b d) -> p b d", b=2)
        pyT = PB[7][:, 0:2 * R].rearrange("p (c n) -> p c n", c=2)
        pao = PB[7][0:R, 0:D]
        pxT = PB[6][0:DC, 0:2 * R].rearrange("p (c n) -> p c n", c=2)
        pg, ppos = PB[7][0:R, 0:E], PB[6][0:R, 0:E]

        for name in ("in_tok", "in_lin", "in_hyena", "in_ffn", "in_fill", "in_exp", "filled", "stored0", "stored1", "scattered0", "scattered1",
                     "in_slots0", "in_slots1", "added", "zeroed", "bf",
                     "dctw", "tokw", "dec", "decb", "fil", "filT", "habs", "hrec", "hT", "hc", "hcoef", "hb",
                     "spec", "sq", "mel", "logmel", "tok", "h0", "st0", "var0", "lnv0", "r0", "u", "uT", "uTs",
                     "z", "zs", "c1", "c2", "conv", "xT", "vT0", "nmax", "ex", "rsum", "v0",
                     "f0", "f1", "prod0", "prod1", "y0", "y1", "g0", "g1", "v1", "v2",
                     "vT", "vTs", "o", "hv", "h1", "st1", "var1", "lnv1", "r1", "xp", "var2", "lnv2", "r2", "an",
                     "aT", "aTs", "k", "qv", "qs", "vs", "kx", "vx0", "vx1", "vx2", "vxs0", "vxs1", "vxs2",
                     "s", "smax", "sc", "es", "psm", "prc", "pn", "pT", "pTs", "yT", "yTs", "ao", "h2", "base",
                     "st2", "var3", "lnv3", "r3", "xl", "xlT", "xlTs", "g", "top", "topi", "diff", "ed", "den",
                     "w0", "meta", "ef", "oh", "chosen", "total", "pos", "slot", "over", "at", "atu",
                     "xeT", "xeTs", "fc", "hid", "pr", "ye", "wfirst", "wab", "wt", "tki"):
            sem(name)

        def need(eng, name, value):
            if value > 0:
                eng.wait_ge(S[name], value)

        block = ctx.enter_context(nc.Block())

        @block.sync
        def _(sp):
            def load(dst, src, name):
                sp.dma_start(dst, src).then_inc(S[name], 16)

            load(dft[:], a["dft"], "in_tok")
            load(melT[:], a["melT"], "in_tok")
            load(dct[:], a["dct"], "in_tok")
            load(wtok[:], a["w_proj"], "in_tok")
            load(tokw[MELS:MELS + 1, :], a["b_proj"], "in_tok")
            load(frames[:], a["frames"], "in_tok")
            load(ident[:], a["ident"], "in_lin")
            load(wlin[:], a["wlin"], "in_lin")
            load(taps[:], a["taps"], "in_lin")
            load(tapb[:], a["tapb"], "in_lin")
            for dst, src in ((hfil, "hfil"), (alph, "alph"), (winb, "winb"), (bmat, "bmat"), (times, "time"),
                             (coef, "coef"), (fwd, "fwd"), (inv, "inv"), (wout, "wout")):
                load(dst[:], a[src], "in_hyena")
            for dst, src in ((ln1, "ln1"), (ln2, "ln2"), (wqkv, "wqkv"), (wo, "wo"), (kmask, "kmask"), (sel, "sel"),
                             (vmask, "vmask"), (causal, "causal"), (before, "before"), (expert, "expert"),
                             (token, "token"), (wgate, "wgate")):
                load(dst[:], a[src], "in_ffn")
            need(sp, "zeroed", 3)
            for e in range(E):
                sp.dma_start(slots[e * CAP:(e + 1) * CAP, :].rearrange("(q p) c -> p q c", p=SR), fill[:])\
                    .then_inc(S["filled"], 16)
            for e in range(E):
                load(wfc[:, e], a["c_fc"][e].rearrange("(k p) f -> p k f", p=DC), "in_exp")
                load(wpr[:, e], a["c_proj_e"][e].rearrange("(m p) d -> p m d", p=128), "in_exp")
            for i in range(NT):
                rows = R if i < NT - 1 else LAST
                need(sp, "base", i + 1)
                sp.dma_start(out[i * R:i * R + rows, :], base[i % 2][0:rows, :]).then_inc(S[f"stored{i % 2}"], 16)
            for p in range(2):
                sp.wait_ge(S[f"scattered{p}"], 16 * TOPK * ((NT + 1 - p) // 2))
            for e in range(E):
                if e >= 2:
                    sp.wait_ge(S["wt"], e - 1)
                    sp.wait_ge(S["xeT"], e - 1)
                    sp.wait_ge(S["tki"], e - 1)
                sp.dma_start(xe[e % 2], slots[e * CAP:(e + 1) * CAP, :].rearrange("(q p) c -> p q c", p=SR))\
                    .then_inc(S[f"in_slots{e % 2}"], 16)
            sp.wait_ge(S["added"], 16 * SQ * E)

        @block.tensor
        def _(pe):
            mm, tr = pe.matmul, pe.transpose

            pe.wait_ge(S["in_tok"], 16 * 6)
            mm(PB[0][0:MELS, 0:D], dct[:], wtok[:], start=True, stop=True).then_inc(S["dctw"], 1)
            pe.wait_ge(S["zeroed"], 3)
            pe.wait_ge(S["tokw"], 1)

            def a_spec(i):
                need(pe, "uTs", i)
                mm(pspec, dft[:], frames[:, i * R:(i + 1) * R], start=True, stop=True).then_inc(S["spec"], 1)

            def a_mel(i):
                pe.wait_ge(S["sq"], i + 1)
                mm(pmel, melT[:], sq[i % 2], start=True, stop=True).then_inc(S["mel"], 1)

            def a_tok(i):
                pe.wait_ge(S["logmel"], i + 1)
                mm(ptok, logmel[i % 2][0:MELS + 1, :], tokw[:], start=True, stop=True).then_inc(S["tok"], 1)

            def a_uT(i):
                if i == 0:
                    pe.wait_ge(S["in_lin"], 16 * 4)
                pe.wait_ge(S["u"], i + 1)
                for k in range(2):
                    last = tr(puT[:, k], u[i % 2][:, k * DC:(k + 1) * DC], ident[0:R, 0:R])
                last.then_inc(S["uT"], 1)

            def a_z(i):
                need(pe, "ex", i)
                need(pe, "v0", i)
                pe.wait_ge(S["uTs"], i + 1)
                for c, m in enumerate(ZC):
                    dst = pz[:, c] if c < 4 else pz4
                    for k in range(2):
                        kk = DC + k
                        last = mm(dst, wlin[0:kk, k, c * 128:c * 128 + m], uT[i % 2][0:kk, k],
                                  start=k == 0, stop=k == 1)
                last.then_inc(S["z"], 1)

            def a_xT(i):
                pe.wait_ge(S["conv"], i + 1)
                for c in range(3):
                    last = tr(px[:, c * 128:(c + 1) * 128], y[i % 2][:, c], ident[:])
                last.then_inc(S["xT"], 1)
                tr(pv[:, 0:128], y[i % 2][:, 3], ident[:])
                tr(pv[:, 128:192], y[i % 2][0:64, 4], ident[0:64, 0:64]).then_inc(S["vT0"], 1)

            def b_f(i, o):
                if i == 0 and o == 0:
                    pe.wait_ge(S["in_hyena"], 16 * 9)
                if o == 0:
                    need(pe, "vTs", i)
                    need(pe, "h1", i)
                pe.wait_ge(S[f"v{o}"], i + 1)
                for c in range(3):
                    last = mm(pf01[:, c * D:(c + 1) * D] if c < 2 else pf2, fwd[:, c], v[i % 2],
                              start=True, stop=True)
                last.then_inc(S[f"f{o}"], 1)

            def b_y(i, o):
                pe.wait_ge(S[f"prod{o}"], i + 1)
                for c in range(3):
                    last = mm(py, inv[:, c], prod[:, c], start=c == 0, stop=c == 2)
                last.then_inc(S[f"y{o}"], 1)

            def b_vT(i):
                pe.wait_ge(S["v2"], i + 1)
                for k in range(2):
                    last = tr(pvT[:, k], v[i % 2][:, k * DC:(k + 1) * DC], ident[0:R, 0:R])
                last.then_inc(S["vT"], 1)

            def b_o(i):
                pe.wait_ge(S["vTs"], i + 1)
                for k in range(2):
                    last = mm(po, vT[i % 2][0:DC + k, k], wout[0:DC + k, k], start=k == 0, stop=k == 1)
                last.then_inc(S["o"], 1)

            def c_aT(i):
                if i == 0:
                    pe.wait_ge(S["in_ffn"], 16 * 12)
                need(pe, "pTs", i)
                pe.wait_ge(S["an"], i + 1)
                for k in range(2):
                    last = tr(paT[:, k], an[i % 2][:, k * DC:(k + 1) * DC], ident[0:R, 0:R])
                last.then_inc(S["aT"], 1)

            def c_qkv(i):
                pe.wait_ge(S["aTs"], i + 1)
                need(pe, "slot", i)
                for n, dst in ((1, pk), (0, pq)):
                    for c, m in ((0, 128), (1, 64)):
                        for k in range(2):
                            last = mm(dst[0:m, c], wqkv[:, k, n * D + c * 128:n * D + c * 128 + m], aT[i % 2][:, k],
                                      start=k == 0, stop=k == 1)
                    if n:
                        last.then_inc(S["k"], 1)
                for k in range(2):
                    last = mm(pvv, aT[i % 2][:, k], wqkv[:, k, 2 * D:], start=k == 0, stop=k == 1)
                last.then_inc(S["qv"], 1)

            def c_vx(i, n):
                if n == 0:
                    need(pe, "topi", i)
                    pe.wait_ge(S["vs"], i + 1)
                else:
                    pe.wait_ge(S[f"vxs{n - 1}"], i + 1)
                for b in range(2 * n, min(2 * n + 2, G)):
                    last = mm(pvx[:, b - 2 * n], sel[:, b], vt[:], start=True, stop=True)
                last.then_inc(S[f"vx{n}"], 1)

            def c_s(i):
                if i == 0:
                    pe.wait_ge(S["bf"], 2)
                pe.wait_ge(S["qs"], i + 1)
                pe.wait_ge(S["kx"], i + 1)
                for g, dst, r0, c in ((0, ps02[:, 0:HG], 0, 0), (1, ps1, 64, 0), (2, ps02[:, HG:2 * HG], 0, 1)):
                    mm(dst, identb[0:R, 0:R], causalb[:], start=True, stop=False)
                    for b in range(G):
                        last = mm(dst, qpad[r0:r0 + GD, c, b], kx[r0:r0 + GD, c, b], start=False, stop=b == G - 1)
                last.then_inc(S["s"], 1)

            def c_pT(i):
                pe.wait_ge(S["pn"], i + 1)
                for g in range(NG):
                    last = tr(ppT[:, g], pn[:, g * HG:(g + 1) * HG], ident[0:R, 0:R])
                last.then_inc(S["pT"], 1)

            def c_yT(i):
                pe.wait_ge(S["pTs"], i + 1)
                pe.wait_ge(S["vxs2"], i + 1)
                for g in range(NG):
                    r0 = GD * (g % 2)
                    for b in range(G):
                        last = mm(pyT[r0:r0 + GD, g // 2, b * T:(b + 1) * T], vx[:, b, g * GD:(g + 1) * GD],
                                  pT[:, g, b * T:(b + 1) * T], start=True, stop=True)
                last.then_inc(S["yT"], 1)

            def c_ao(i):
                pe.wait_ge(S["yTs"], i + 1)
                mm(pao, yT[:, 0], wo[:, 0], start=True, stop=False)
                mm(pao, yT[0:64, 1], wo[0:64, 1], start=False, stop=True).then_inc(S["ao"], 1)

            def c_xlT(i):
                pe.wait_ge(S["xl"], i + 1)
                for k in range(2):
                    last = tr(pxT[:, k], xl[i % 2][:, k * DC:(k + 1) * DC], ident[0:R, 0:R])
                last.then_inc(S["xlT"], 1)

            def c_gate(i):
                pe.wait_ge(S["xlTs"], i + 1)
                for k in range(2):
                    last = mm(pg, xlT[:, k], wgate[:, k], start=k == 0, stop=k == 1)
                last.then_inc(S["g"], 1)

            def c_pos(i):
                pe.wait_ge(S["chosen"], i + 1)
                need(pe, "total", i)
                last = mm(ppos, beforeb[:], chosen[i % 2], start=True, stop=i == 0)
                if i:
                    last = mm(ppos, onesb[:], total[(i - 1) % 2], start=False, stop=True)
                last.then_inc(S["pos"], 1)

            def filters():
                pe.wait_ge(S["fil"], 2)
                for o in range(2):
                    for k in range(2):
                        last = tr(PB[7][0:T, o * D + k * DC:o * D + (k + 1) * DC], hfil[:, o, k], ident[0:DC, 0:DC])
                last.then_inc(S["filT"], 1)
                pe.wait_ge(S["hT"], 2)
                pe.wait_ge(S["hb"], 1)
                for o in range(2):
                    if o:
                        pe.wait_ge(S["hcoef"], 1)
                    for c in range(3):
                        last = mm((pf01[:, c * D:(c + 1) * D] if c < 2 else pf2), coef[:, c], hT[:, o],
                                  start=True, stop=True)
                    last.then_inc(S["hc"], 1)
                pe.wait_ge(S["hcoef"], 2)

            for j in range(NT + 2):
                A, Bt, C = j < NT, 0 <= j - 1 < NT, 0 <= j - 2 < NT
                i, b, c = j, j - 1, j - 2
                if C: c_aT(c)
                if A: a_spec(i)
                if Bt: b_f(b, 0)
                if C: c_qkv(c)
                if A: a_mel(i)
                if Bt: b_y(b, 0)
                if C: c_vx(c, 0)
                if C: c_s(c)
                if A: a_tok(i)
                if j == 0:
                    pe.wait_ge(S["in_hyena"], 16 * 9)
                    filters()
                if C: c_vx(c, 1)
                if Bt: b_f(b, 1)
                if C: c_vx(c, 2)
                if A: a_uT(i)
                if Bt: b_y(b, 1)
                if C: c_pT(c)
                if A: a_z(i)
                if C: c_yT(c)
                if Bt: b_vT(b)
                if C: c_ao(c)
                if A: a_xT(i)
                if Bt: b_o(b)
                if C: c_xlT(c)
                if C: c_gate(c)
                if C: c_pos(c)

            def e_xT(e):
                need(pe, "xeTs", e)
                pe.wait_ge(S[f"in_slots{e % 2}"], 16 * (e // 2 + 1))
                for k in range(2):
                    for q in range(SQ):
                        last = tr(PB[k][0:DC, q * SR:(q + 1) * SR], xe[e % 2][:, q, k * DC:(k + 1) * DC],
                                  ident[0:SR, 0:SR])
                last.then_inc(S["xeT"], 1)

            def e_fc(e):
                pe.wait_ge(S["xeTs"], e + 1)
                for m in range(MC):
                    n = e * MC + m
                    need(pe, "hid", n - 3)
                    for k in range(2):
                        last = mm(PB[2 + n % 4][:, 0:CAP], wfc[:, e, k, m * 128:(m + 1) * 128], xeT[e % 2][:, k],
                                  start=k == 0, stop=k == 1)
                    last.then_inc(S["fc"], 1)

            def e_pr(e):
                for q in range(SQ):
                    if q % 2 == 0:
                        need(pe, "ye", SQ * (e - 1) + q + 2)
                    for m in range(MC):
                        if q == 0:
                            pe.wait_ge(S["hid"], e * MC + m + 1)
                        last = mm(PB[6 + q // 2][0:SR, (q % 2) * D:(q % 2 + 1) * D],
                                  hid[e % 2][:, m, q * SR:(q + 1) * SR], wpr[:, e, m], start=m == 0, stop=m == MC - 1)
                    last.then_inc(S["pr"], 1)

            pe.wait_ge(S["in_exp"], 16 * 2 * E)
            pe.wait_ge(S["slot"], NT)
            e_xT(0)
            for e in range(E):
                e_fc(e)
                if e + 1 < E:
                    e_xT(e + 1)
                e_pr(e)

        @block.scalar
        def _(act):
            f = act.activation

            def rstd_of(name, n, src, i):
                act.wait_ge(S[{0: "var0", 1: "var1", 2: "var2", 3: "var3"}[n]], i + 1)
                f(lnv[:, n:n + 1], src, ACT.Ln, bias=epsc[0:R, 0:1]).then_inc(S[f"lnv{n}"], 1)
                act.wait_ge(S[f"lnv{n}"], i + 1)
                f(rstd[:, n:n + 1], lnv[:, n:n + 1], ACT.Exp, scale=-0.5).then_inc(S[f"r{n}"], 1)

            act.wait_ge(S["zeroed"], 3)
            act.wait_ge(S["dctw"], 1)
            f(tokw[0:MELS, :], PB[0][0:MELS, 0:D], ACT.Copy).then_inc(S["tokw"], 1)

            def a_sq(i):
                act.wait_ge(S["spec"], i + 1)
                need(act, "mel", i - 1)
                f(sq[i % 2], pspec, ACT.Square).then_inc(S["sq"], 1)

            def a_log(i):
                act.wait_ge(S["mel"], i + 1)
                need(act, "tok", i - 1)
                f(logmel[i % 2][0:MELS, :], pmel, ACT.Ln, bias=epsc[0:MELS, 1:2]).then_inc(S["logmel"], 1)

            def a_h0(i):
                act.wait_ge(S["tok"], i + 1)
                need(act, "hv", i - 1)
                f(h0[i % 2], ptok, ACT.Copy).then_inc(S["h0"], 1)

            def a_r(i):
                rstd_of("0", 0, mv[:, 0, 1:2], i)

            def a_uTs(i):
                act.wait_ge(S["uT"], i + 1)
                need(act, "z", i - 1)
                f(uT[i % 2][0:DC], puT, ACT.Copy).then_inc(S["uTs"], 1)

            def a_zs(i):
                act.wait_ge(S["z"], i + 1)
                need(act, "conv", i - 1)
                for c in range(4):
                    f(z[i % 2][:, c, :, KW - 1:], pz[:, c].rearrange("p (b t) -> p b t", t=T), ACT.Copy)
                f(z[i % 2][0:64, 4, :, KW - 1:], pz4.rearrange("p (b t) -> p b t", t=T), ACT.Copy)\
                    .then_inc(S["zs"], 1)

            def a_ex(i):
                act.wait_ge(S["nmax"], i + 1)
                need(act, "g1", i - 1)
                need(act, "rsum", i - 1)
                for o in range(2):
                    last = f(ex[i % 2][:, o], px[:, o * D:(o + 1) * D], ACT.Exp, bias=nmax[i % 2][:, o:o + 1],
                             accum_out=ssum[i % 2][:, o:o + 1])
                last.then_inc(S["ex"], 1)

            def b_vTs(i):
                act.wait_ge(S["vT"], i + 1)
                need(act, "o", i - 1)
                f(vT[i % 2][0:DC], pvT, ACT.Copy).then_inc(S["vTs"], 1)

            def b_r(i):
                rstd_of("1", 1, mv[:, 1, 1:2], i)

            def b_r2(i):
                rstd_of("2", 2, var2[:], i)

            def c_aTs(i):
                if i == 0:
                    act.wait_ge(S["in_ffn"], 16 * 12)
                act.wait_ge(S["aT"], i + 1)
                need(act, "qv", i - 1)
                for k in range(2):
                    last = f(aT[i % 2][:, k], paT[:, k], ACT.Copy, scale=ln1[:, k:k + 1])
                last.then_inc(S["aTs"], 1)

            def c_qs(i):
                act.wait_ge(S["qv"], i + 1)
                need(act, "s", i)
                for c, m in ((0, 128), (1, 64)):
                    flat = qpad[0:m, c].rearrange("p b n -> p (b n)")
                    for b in range(G):
                        last = f(flat[:, b * (R + T):b * (R + T) + T], pq[0:m, c, b * T:(b + 1) * T], ACT.Copy)
                last.then_inc(S["qs"], 1)

            def c_vs(i):
                act.wait_ge(S["qv"], i + 1)
                need(act, "vx2", i)
                f(vt[:], pvv, ACT.Copy).then_inc(S["vs"], 1)

            def c_es(i):
                act.wait_ge(S["sc"], i + 1)
                need(act, "pn", i)
                f(es[:], sc[:], ACT.Exp, scale=SCALE).then_inc(S["es"], 1)

            def c_pTs(i):
                act.wait_ge(S["pT"], i + 1)
                need(act, "yT", i)
                f(pT[:], ppT, ACT.Copy).then_inc(S["pTs"], 1)

            def c_yTs(i):
                act.wait_ge(S["yT"], i + 1)
                need(act, "ao", i)
                f(yT[:, 0], pyT[:, 0], ACT.Copy)
                f(yT[0:64, 1], pyT[0:64, 1], ACT.Copy).then_inc(S["yTs"], 1)

            def c_r(i):
                rstd_of("3", 3, mv[:, 2, 1:2], i)

            def c_xlTs(i):
                act.wait_ge(S["xlT"], i + 1)
                need(act, "g", i)
                for k in range(2):
                    last = f(xlT[:, k], pxT[:, k], ACT.Copy, scale=ln2[:, k:k + 1])
                last.then_inc(S["xlTs"], 1)

            def c_ed(i):
                act.wait_ge(S["diff"], i + 1)
                need(act, "w0", i)
                f(ed[:], diff[:], ACT.Exp).then_inc(S["ed"], 1)

            def filters():
                act.wait_ge(S["in_hyena"], 16 * 9)
                for k in range(2):
                    last = f(hdec[:, k], times[:], ACT.Exp, scale=alph[:, k:k + 1])
                last.then_inc(S["dec"], 1)

            for j in range(NT + 2):
                A, Bt, C = j < NT, 0 <= j - 1 < NT, 0 <= j - 2 < NT
                i, b, c = j, j - 1, j - 2
                if C: c_aTs(c)
                if A: a_sq(i)
                if C: c_qs(c)
                if C: c_vs(c)
                if A: a_log(i)
                if j == 0: filters()
                if A: a_h0(i)
                if A: a_r(i)
                if C: c_es(c)
                if A: a_uTs(i)
                if C: c_pTs(c)
                if A: a_zs(i)
                if Bt: b_vTs(b)
                if C: c_yTs(c)
                if A: a_ex(i)
                if C: c_r(c)
                if Bt: b_r(b)
                if Bt: b_r2(b)
                if C: c_xlTs(c)
                if C: c_ed(c)

            for e in range(E):
                for m in range(MC):
                    n = e * MC + m
                    act.wait_ge(S["fc"], n + 1)
                    if m == 0:
                        need(act, "pr", SQ * (e - 1))
                    f(hid[e % 2][:, m], PB[2 + n % 4][:, 0:CAP], ACT.Gelu).then_inc(S["hid"], 1)

        @block.vector
        def _(ve):
            tt, ts, stt = ve.tensor_tensor, ve.tensor_scalar, ve.scalar_tensor_tensor

            def layer_stats(n, src, i, var):
                ve.bn_stats(stat[:, n], src).then_inc(S[f"st{n}"], 1)
                ve.wait_ge(S[f"st{n}"], i + 1)
                ve.bn_aggr(mv[:, n], stat[:, n]).then_inc(S[var], 1)

            def a_stats(i):
                ve.wait_ge(S["h0"], i + 1)
                layer_stats(0, h0[i % 2], i, "var0")

            def a_u(i):
                ve.wait_ge(S["r0"], i + 1)
                need(ve, "uT", i - 1)
                ts(u[i % 2], h0[i % 2], mv[:, 0, 0:1], rstd[:, 0:1], ALU.subtract, ALU.mult).then_inc(S["u"], 1)

            def a_conv(i):
                ve.wait_ge(S["zs"], i + 1)
                need(ve, "vT0", i - 1)
                yv = [y[i % 2][0:ZC[c], c].rearrange("p (b t) -> p b t", t=T) for c in range(5)]
                zv = lambda c, k: z[i % 2][0:ZC[c], c, :, k:k + T]
                for c in range(5):
                    m = ZC[c]
                    last = ts(yv[c], zv(c, 0), taps[0:m, c, 0:1], tapb[0:m, c:c + 1], ALU.mult, ALU.add)
                last.then_inc(S["c1"], 1)
                ve.wait_ge(S["c1"], i + 1)
                for c in range(5):
                    last = stt(yv[c], zv(c, 1), taps[0:ZC[c], c, 1:2], yv[c], ALU.mult, ALU.add)
                last.then_inc(S["c2"], 1)
                ve.wait_ge(S["c2"], i + 1)
                for c in range(5):
                    last = stt(yv[c], zv(c, 2), taps[0:ZC[c], c, 2:3], yv[c], ALU.mult, ALU.add)
                last.then_inc(S["conv"], 1)

            def a_nmax(i):
                ve.wait_ge(S["xT"], i + 1)
                ve.tensor_reduce(nmax[i % 2], px.rearrange("p (o d) -> p o d", o=2), AX.X, ALU.max, negate=True)\
                    .then_inc(S["nmax"], 1)

            def a_v0(i):
                ve.wait_ge(S["vT0"], i + 1)
                need(ve, "vT", i - 1)
                need(ve, "hv", i - 1)
                tt(v[i % 2], pv, u[i % 2], ALU.add).then_inc(S["v0"], 1)

            def a_rsum(i):
                ve.wait_ge(S["ex"], i + 1)
                ve.reciprocal(rsum[i % 2], ssum[i % 2]).then_inc(S["rsum"], 1)

            def b_prod(i, o):
                ve.wait_ge(S[f"f{o}"], i + 1)
                if o == 1:
                    ve.wait_ge(S["y0"], i + 1)
                else:
                    need(ve, "y1", i)
                tt(prod[:, 0:2].rearrange("p c d -> p (c d)"), pf01,
                   hcoef[:, o, 0:2].rearrange("p c d -> p (c d)"), ALU.mult)
                tt(prod[:, 2], pf2, hcoef[:, o, 2], ALU.mult).then_inc(S[f"prod{o}"], 1)

            def b_v(i, o):
                ve.wait_ge(S[f"y{o}"], i + 1)
                ve.wait_ge(S["rsum"], i + 1)
                stt(gate[:], ex[i % 2][:, o], rsum[i % 2][:, o:o + 1], py, ALU.mult, ALU.mult)\
                    .then_inc(S[f"g{o}"], 1)
                ve.wait_ge(S[f"g{o}"], i + 1)
                tt(v[i % 2], v[i % 2], gate[:], ALU.add).then_inc(S[f"v{o + 1}"], 1)

            def b_h1(i):
                ve.wait_ge(S["o"], i + 1)
                ve.wait_ge(S["hv"], i + 1)
                need(ve, "base", i - 1)
                tt(h1[i % 2], po, hv[:], ALU.add).then_inc(S["h1"], 1)
                ve.wait_ge(S["h1"], i + 1)
                layer_stats(1, h1[i % 2], i, "var1")

            def b_xp(i):
                ve.wait_ge(S["r1"], i + 1)
                stt(var2[:], mv[:, 1, 1:2], rstd[:, 1:2], rstd[:, 1:2], ALU.mult, ALU.mult).then_inc(S["var2"], 1)
                ts(xp[i % 2], h1[i % 2], mv[:, 1, 0:1], rstd[:, 1:2], ALU.subtract, ALU.mult).then_inc(S["xp"], 1)

            def b_an(i):
                ve.wait_ge(S["xp"], i + 1)
                ve.wait_ge(S["r2"], i + 1)
                need(ve, "aT", i - 1)
                ts(an[i % 2], xp[i % 2], rstd[:, 2:3], None, ALU.mult).then_inc(S["an"], 1)

            def c_kx(i):
                if i == 0:
                    ve.wait_ge(S["in_ffn"], 16 * 12)
                ve.wait_ge(S["k"], i + 1)
                need(ve, "s", i)
                for c, m in ((0, 128), (1, 64)):
                    src = pk[0:m, c].rearrange("p (b k) -> p b k", k=T)[:, :, None, :].broadcast_to([m, G, HG, T])
                    msk = kmask[0:m].rearrange("p (h k) -> p h k", k=T)[:, None].broadcast_to([m, G, HG, T])
                    last = tt(kx[0:m, c].rearrange("p b (h k) -> p b h k", k=T), src, msk, ALU.mult)
                last.then_inc(S["kx"], 1)

            def c_vxs(i, n):
                if n == 0:
                    need(ve, "yT", i)
                ve.wait_ge(S[f"vx{n}"], i + 1)
                k = min(2, G - 2 * n)
                tt(vx[:, 2 * n:2 * n + k], pvx[:, 0:k], vmask[:, None, :].broadcast_to([HG * T, k, D]), ALU.mult)\
                    .then_inc(S[f"vxs{n}"], 1)

            SCORES = ((ps02[:, 0:HG], slice(0, HG)), (ps1, slice(HG, 2 * HG)), (ps02[:, HG:2 * HG], slice(2 * HG, 3 * HG)))

            def c_sc(i):
                ve.wait_ge(S["s"], i + 1)
                for src, hs in SCORES:
                    last = ve.tensor_reduce(smax[:, hs], src, AX.X, ALU.max)
                last.then_inc(S["smax"], 1)
                ve.wait_ge(S["smax"], i + 1)
                need(ve, "es", i)
                for src, hs in SCORES:
                    last = tt(sc[:, hs], src, smax[:, hs, None].broadcast_to([R, HG, T]), ALU.subtract)
                last.then_inc(S["sc"], 1)

            def c_pn(i):
                ve.wait_ge(S["es"], i + 1)
                ve.tensor_reduce(psm[:], es[:], AX.X, ALU.add).then_inc(S["psm"], 1)
                ve.wait_ge(S["psm"], i + 1)
                ve.reciprocal(prc[:], psm[:]).then_inc(S["prc"], 1)
                ve.wait_ge(S["prc"], i + 1)
                need(ve, "pT", i)
                tt(pn[:], es[:], prc[:, :, None].broadcast_to([R, HEADS, T]), ALU.mult).then_inc(S["pn"], 1)

            def c_h2(i):
                ve.wait_ge(S["ao"], i + 1)
                need(ve, "base", i - 1)
                tt(h2[i % 2], pao, xp[i % 2], ALU.add).then_inc(S["h2"], 1)
                ve.wait_ge(S["h2"], i + 1)
                layer_stats(2, h2[i % 2], i, "var3")

            def c_xl(i):
                ve.wait_ge(S["r3"], i + 1)
                if i >= 2:
                    ve.wait_ge(S[f"scattered{i % 2}"], 16 * TOPK * (i // 2))
                need(ve, "xlT", i - 1)
                ts(xl[i % 2][:, 0:D], h2[i % 2], mv[:, 2, 0:1], rstd[:, 3:4], ALU.subtract, ALU.mult)\
                    .then_inc(S["xl"], 1)

            def c_route(i):
                p = i % 2
                ve.wait_ge(S["g"], i + 1)
                ve.max(top[p], pg).then_inc(S["top"], 1)
                ve.wait_ge(S["top"], i + 1)
                ve.max_index(topi[p], top[p], pg).then_inc(S["topi"], 1)
                tt(diff[:], top[p][:, 1:2], top[p][:, 0:1], ALU.subtract).then_inc(S["diff"], 1)
                ve.wait_ge(S["topi"], i + 1)
                ve.tensor_copy(ef[p], topi[p][:, 0:2]).then_inc(S["ef"], 1)
                ve.wait_ge(S["ef"], i + 1)
                for k in range(2):
                    last = ts(oh[:, k], expert[0:R], ef[p][:, k:k + 1], None, ALU.is_equal)
                last.then_inc(S["oh"], 1)
                ve.wait_ge(S["oh"], i + 1)
                need(ve, "pos", i - 1)
                tt(chosen[p], oh[:, 0], oh[:, 1], ALU.add).then_inc(S["chosen"], 1)
                ve.wait_ge(S["chosen"], i + 1)
                if i == 0:
                    ve.tensor_copy(total[0], chosen[0]).then_inc(S["total"], 1)
                else:
                    tt(total[p], total[1 - p], chosen[p], ALU.add).then_inc(S["total"], 1)

            def c_slots(i):
                p = i % 2
                ve.wait_ge(S["ed"], i + 1)
                ts(den[:], ed[:], 1.0, None, ALU.add).then_inc(S["den"], 1)
                ve.wait_ge(S["den"], i + 1)
                ve.reciprocal(xl[p][:, D + 2:D + 3], den[:]).then_inc(S["w0"], 1)
                ve.wait_ge(S["w0"], i + 1)
                tt(xl[p][:, D + 3:D + 4], ed[:], xl[p][:, D + 2:D + 3], ALU.mult)
                ve.tensor_copy(xl[p][:, D + 1:D + 2], ef[p][:, 0:1])
                ve.tensor_copy(xl[p][:, D:D + 1], token[:, i:i + 1]).then_inc(S["meta"], 1)
                ve.wait_ge(S["pos"], i + 1)
                for k in range(2):
                    last = ve.tensor_tensor_reduce(junk[:, k], ppos, oh[:, k], 1.0, 0.0, ALU.mult, ALU.add,
                                                   slot[:, k:k + 1])
                last.then_inc(S["slot"], 1)
                ve.wait_ge(S["slot"], i + 1)
                ts(over[:], slot[:], float(CAP), NOWHERE, ALU.is_ge, ALU.mult).then_inc(S["over"], 1)
                stt(at[:], ef[p], float(CAP), slot[:], ALU.mult, ALU.add)
                ve.wait_ge(S["over"], i + 1)
                tt(slot[:], over[:], slot[:], ALU.add).then_inc(S["at"], 1)
                ve.wait_ge(S["at"], i + 1)
                stt(atu[p], ef[p], float(CAP), slot[:], ALU.mult, ALU.add).then_inc(S["atu"], 1)

            ve.memset(epsc[:, 0:1], EPS)
            ve.memset(epsc[:, 1:2], 1e-6)
            for p in range(2):
                ve.memset(logmel[p], 1.0)
                ve.memset(uT[p], 1.0)
                ve.memset(vT[p], 1.0)
                ve.memset(z[p], 0.0)
            ve.memset(qpad[:], 0.0)
            ve.memset(onesb[:], 1.0).then_inc(S["zeroed"], 1)
            ve.memset(fill[:], 0.0).then_inc(S["zeroed"], 1)
            ve.wait_ge(S["zeroed"], 2)
            ve.memset(fill[:, :, D:D + 1], NOWHERE).then_inc(S["zeroed"], 1)

            def filters():
                ve.wait_ge(S["dec"], 1)
                for k in range(2):
                    last = ts(hdec[:, k], hdec[:, k], winb[:, k:k + 1], None, ALU.add)
                last.then_inc(S["decb"], 1)
                ve.wait_ge(S["decb"], 1)
                for o in range(2):
                    tt(hfil[:, o], hfil[:, o], hdec[:], ALU.mult).then_inc(S["fil"], 1)
                ve.wait_ge(S["filT"], 1)
                src = PB[7][0:T, 0:2 * D].rearrange("p (o d) -> p o d", o=2)
                ve.tensor_reduce(habs[:], src, AX.X, ALU.add, apply_absolute_value=True).then_inc(S["habs"], 1)
                ve.wait_ge(S["habs"], 1)
                ve.reciprocal(hrec[:], habs[:]).then_inc(S["hrec"], 1)
                ve.wait_ge(S["hrec"], 1)
                for o in range(2):
                    ts(hT[:, o], src[:, o], hrec[:, o:o + 1], None, ALU.mult).then_inc(S["hT"], 1)
                ve.wait_ge(S["hT"], 2)
                tt(hT[0:1], hT[0:1], bmat[:], ALU.add).then_inc(S["hb"], 1)
                for o in range(2):
                    ve.wait_ge(S["hc"], o + 1)
                    ve.tensor_copy(hcoef[:, o, 0:2].rearrange("p c d -> p (c d)"), pf01)
                    ve.tensor_copy(hcoef[:, o, 2], pf2).then_inc(S["hcoef"], 1)

            for j in range(NT + 2):
                A, Bt, C = j < NT, 0 <= j - 1 < NT, 0 <= j - 2 < NT
                i, b, c = j, j - 1, j - 2
                if C: c_kx(c)
                if Bt: b_prod(b, 0)
                if A: a_stats(i)
                if C: c_vxs(c, 0)
                if Bt: b_v(b, 0)
                if C: c_sc(c)
                if C: c_vxs(c, 1)
                if A: a_u(i)
                if j == 0: filters()
                if Bt: b_prod(b, 1)
                if C: c_pn(c)
                if C: c_vxs(c, 2)
                if Bt: b_v(b, 1)
                if A: a_conv(i)
                if C: c_h2(c)
                if A: a_v0(i)
                if A: a_nmax(i)
                if Bt: b_h1(b)
                if C: c_xl(c)
                if Bt: b_xp(b)
                if Bt: b_an(b)
                if A: a_rsum(i)
                if C: c_route(c)
                if C: c_slots(c)
                if j == 2:
                    pass
                if j == 0:
                    ve.wait_ge(S["in_ffn"], 16 * 12)
                    ve.tensor_copy(causalb[:], causal[:])
                    ve.tensor_copy(beforeb[:], before[:]).then_inc(S["bf"], 1)
                    ve.wait_ge(S["in_lin"], 16 * 4)
                    ve.tensor_copy(identb[:], ident[:]).then_inc(S["bf"], 1)

            def e_xTs(e):
                ve.wait_ge(S["xeT"], e + 1)
                need(ve, "fc", MC * (e - 1))
                for k in range(2):
                    last = ts(xeT[e % 2][:, k], PB[k][0:DC, 0:CAP], ln2[:, k:k + 1], None, ALU.mult)
                last.then_inc(S["xeTs"], 1)

            def e_meta(e):
                x = xe[e % 2]
                ve.wait_ge(S[f"in_slots{e % 2}"], 16 * (e // 2 + 1))
                if e >= 2:
                    ve.wait_ge(S["added"], 16 * SQ * (e - 1))
                ve.tensor_copy(tok[e % 2], x[:, :, D]).then_inc(S["tki"], 1)
                ts(first[:], x[:, :, D + 1], float(e), None, ALU.is_equal).then_inc(S["wfirst"], 1)
                ve.wait_ge(S["wfirst"], e + 1)
                tt(wa[:], first[:], x[:, :, D + 2], ALU.mult)
                stt(wb[:], first[:], 0.0, x[:, :, D + 3], ALU.is_equal, ALU.mult).then_inc(S["wab"], 1)
                ve.wait_ge(S["wab"], e + 1)
                tt(wt[e % 2], wa[:], wb[:], ALU.add).then_inc(S["wt"], 1)

            e_xTs(0)
            e_meta(0)
            for e in range(E):
                if e + 1 < E:
                    e_xTs(e + 1)
                    e_meta(e + 1)
                ve.wait_ge(S["wt"], e + 1)
                if e >= 2:
                    ve.wait_ge(S["added"], 16 * SQ * (e - 1))
                for q in range(SQ):
                    ve.wait_ge(S["pr"], SQ * e + q // 2 * 2 + 2)
                    ts(ye[e % 2][:, q], PB[6 + q // 2][0:SR, (q % 2) * D:(q % 2 + 1) * D], wt[e % 2][:, q:q + 1],
                       None, ALU.mult).then_inc(S["ye"], 1)

        @block.gpsimd
        def _(pool):
            def b_hv(i):
                pool.wait_ge(S["v2"], i + 1)
                pool.wait_ge(S["h0"], i + 1)
                need(pool, "h1", i)
                pool.tensor_tensor(hv[:], v[i % 2], h0[i % 2], ALU.add).then_inc(S["hv"], 1)

            def c_base(i):
                pool.wait_ge(S["h2"], i + 1)
                pool.wait_ge(S["h1"], i + 1)
                if i >= 2:
                    pool.wait_ge(S[f"stored{i % 2}"], 16 * (i // 2))
                pool.tensor_tensor(base[i % 2], h2[i % 2], h1[i % 2], ALU.add).then_inc(S["base"], 1)

            def c_scatter(i):
                rows = R if i < NT - 1 else LAST
                if i == 0:
                    pool.wait_ge(S["filled"], 16 * E)
                pool.wait_ge(S["meta"], i + 1)
                pool.wait_ge(S["atu"], i + 1)
                for k in range(TOPK):
                    pool.indirect_dma_start(
                        slots, bass.IndirectOffsetOnAxis(ap=atu[i % 2][0:rows, k:k + 1], axis=0),
                        xl[i % 2][0:rows, :], None, bounds_check=E * CAP - 1, oob_is_err=False)\
                        .then_inc(S[f"scattered{i % 2}"], 16)

            for j in range(NT + 2):
                Bt, C = 0 <= j - 1 < NT, 0 <= j - 2 < NT
                if C: c_base(j - 2)
                if Bt: b_hv(j - 1)
                if C: c_scatter(j - 2)

            for p in range(2):
                pool.wait_ge(S[f"stored{p}"], 16 * ((NT + 1 - p) // 2))
            for e in range(E):
                if e:
                    pool.wait_ge(S["added"], 16 * SQ * e)
                for q in range(SQ):
                    pool.wait_ge(S["ye"], SQ * e + q + 1)
                    pool.indirect_dma_start(
                        out, bass.IndirectOffsetOnAxis(ap=tok[e % 2][:, q:q + 1], axis=0),
                        ye[e % 2][:, q], None, bounds_check=TOKENS - 1, oob_is_err=False,
                        compute_op=ALU.add).then_inc(S["added"], 16)


def layout(x, i):
    import numpy as np
    d = {k: np.asarray(w) for k, w in i.items()}
    x = np.asarray(x)
    o = {}
    order = np.minimum(np.arange(NT * G), B - 1)
    fr = np.stack([x[:, n * HOP:n * HOP + FRAME] for n in range(T)], 1)[order]
    o["frames"] = fr.reshape(NT * R, FRAME).T
    mel = d["L0_tok_mel_filters"].T
    o["melT"] = np.concatenate([mel, mel], 0)
    o["dct"] = d["L0_tok_dct"]
    o["w_proj"] = d["L0_tok_w_proj"]
    o["b_proj"] = d["L0_tok_b_proj"][None]

    def chunks(w, extra=None):
        w = w.reshape(2, DC, -1).transpose(1, 0, 2)
        if extra is not None:
            w = np.concatenate([w, np.broadcast_to(extra, (1, 2, w.shape[2]))], 0)
        return w

    o["wlin"] = chunks(d["L0_attn_W_lin"].T, d["L0_attn_b_lin"])
    pad = lambda w: np.concatenate([w, np.zeros((5 * 128 - 3 * D,) + w.shape[1:], w.dtype)], 0)
    o["taps"] = pad(d["L0_attn_conv_w"][:, 0]).reshape(5, 128, KW).transpose(1, 0, 2)
    o["tapb"] = pad(d["L0_attn_conv_b"]).reshape(5, 128).T
    o["hfil"] = d["L0_attn_h_param"][:, :, :T].reshape(2, 2, DC, T).transpose(2, 0, 1, 3)
    o["alph"] = d["L0_attn_alphas"].reshape(2, DC).T
    o["winb"] = d["L0_attn_win_b"].reshape(2, DC).T
    o["bmat"] = d["L0_attn_Bmat"].reshape(1, 2, D)
    o["wout"] = chunks(d["L0_attn_W_out"].T, d["L0_attn_b_out"])
    o["ln1"] = d["L0_ffn_ln1_w"].reshape(2, DC).T
    o["ln2"] = d["L0_ffn_ln2_w"].reshape(2, DC).T
    o["wqkv"] = chunks(d["L0_ffn_c_attn_w"].T)
    w = d["L0_ffn_c_proj_w"].T
    o["wo"] = np.concatenate([w, np.zeros((64, D), w.dtype)], 0).reshape(2, 128, D).transpose(1, 0, 2)
    o["wgate"] = chunks(d["L0_ffn_w_g"].T)
    o["c_fc"] = d["L0_ffn_c_fc"]
    o["c_proj_e"] = d["L0_ffn_c_proj_e"]
    return o


SHAPES = {"fwd": (R, 3, FC), "coef": (T, 3, FC), "inv": (FC, 3, R), "sel": (R, G, HG * T)}


def kernel(x, **inputs):
    import numpy as np
    import concourse.bacc as bacc
    from concourse.bass_utils import run_bass_kernel_spmd

    nc = bacc.Bacc("TRN2", target_bir_lowering=False, num_devices=1)
    arrays, a = {}, {}
    for name, value in {**layout(x, inputs), **constants()}.items():
        value = np.ascontiguousarray(value).reshape(SHAPES.get(name, value.shape))
        arrays["in_" + name] = value
        a[name] = nc.dram_tensor("in_" + name, value.shape, mybir.dt.from_np(value.dtype), kind="ExternalInput").ap()
    out = nc.dram_tensor("out_0", (TOKENS, D), F32, kind="ExternalOutput").ap()
    tower(nc, a, out)
    r = run_bass_kernel_spmd(nc, [arrays], core_ids=[0])
    return r.results[0]["out_0"].reshape(B, T, D)
```

```python
from contextlib import ExitStack

import concourse.bass as bass
from concourse import mybir

ALU = mybir.AluOpType
ACT = mybir.ActivationFunctionType
AX = mybir.AxisListType
F32 = mybir.dt.float32
BF16 = mybir.dt.bfloat16
U32 = mybir.dt.uint32

B, T, D = 64, 25, 192
G = 5
R = G * T
NT = -(-B // G)
LAST = (B - (NT - 1) * G) * T
TOKENS = B * T
FRAME, HOP, BINS, MELS, MFCC = 100, 160, 51, 40, 13
DC = D // 2
LANES = 6
KW = 3
ZC = [128, 128, 128, 128, 64]
NF = 2 * T - 1
FR = 3 * (NF // 2) + 1
FC = -(-G * FR // 3)
HEADS, HD = 12, 16
HG = 4
NG = HEADS // HG
GD = HG * HD
E, TOPK, FF = 8, 2, 4 * D
CAP = TOPK * TOKENS // E
SQ = 4
SR = CAP // SQ
MC = FF // 128
ROW = D + 4
NOWHERE = float(1 << 22)
EPS = 1e-5
SCALE = HD ** -0.5
MASKED = -1e30


def constants():
    import numpy as np
    c = {}
    n = np.arange(FRAME)
    window = 0.54 - 0.46 * np.cos(2.0 * np.pi * n / (FRAME - 1))
    ang = 2.0 * np.pi * np.outer(n, np.arange(BINS)) / FRAME
    c["dft"] = np.concatenate([np.cos(ang), -np.sin(ang)], 1) * window[:, None]
    t = np.arange(T)
    fwd, coef, inv = [np.ones(T)], [np.ones(T)], [np.ones(T) / NF]
    for f in range(1, NF // 2 + 1):
        co, si = np.cos(2 * np.pi * f * t / NF), np.sin(2 * np.pi * f * t / NF)
        fwd += [co - si, co, -si]
        coef += [co, -si - co, co - si]
        inv += [2 * (co - si) / NF, -2 * si / NF, -2 * co / NF]
    fwd, coef, inv = np.array(fwd), np.array(coef), np.array(inv)
    A = np.zeros((R, 3 * FC)); H = np.zeros((T, 3 * FC)); V = np.zeros((3 * FC, R))
    for b in range(G):
        r, k = slice(b * T, b * T + T), slice(b * FR, b * FR + FR)
        A[r, k] = fwd.T
        H[:, k] = coef.T
        V[k, r] = inv
    c["fwd"], c["coef"] = A, H
    c["inv"] = V.reshape(3, FC, R).transpose(1, 0, 2).reshape(FC, 3 * R)
    c["time"] = np.tile(np.linspace(0.0, 1.0, 512, dtype=np.float32)[:T], (DC, 1))
    c["ident"] = np.eye(128)
    head_of_row = (np.arange(128) % GD) // HD
    c["kmask"] = (head_of_row[:, None] == np.repeat(np.arange(HG), T)[None]) * 1.0
    sel = np.zeros((R, G, HG * T))
    for b in range(G):
        for h in range(HG):
            for k in range(T):
                sel[b * T + k, b, h * T + k] = 1.0
    c["sel"] = sel.reshape(R, -1)
    vh = (np.arange(D) % GD) // HD
    c["vmask"] = (np.repeat(np.arange(HG), T)[:, None] == vh[None]) * 1.0
    q = np.arange(R) % T
    c["causal"] = np.where(np.tile(np.arange(T), HG)[None] > q[:, None], MASKED, 0.0)
    c["before"] = (np.arange(R)[:, None] < np.arange(R)[None]) * 1.0
    c["expert"] = np.tile(np.arange(E), (128, 1))
    c["token"] = np.arange(R)[:, None] + R * np.arange(NT)[None]
    return {k: np.ascontiguousarray(v, dtype=np.float32) for k, v in c.items()}


def tower(nc, a, out):
    with ExitStack() as ctx:
        def sb(name, shape, dt=F32):
            return ctx.enter_context(nc.sbuf_tensor(name, shape, dt))

        S = {}

        def sem(name):
            S[name] = ctx.enter_context(nc.semaphore("s_" + name))
            return S[name]

        slots = nc.dram_tensor("slots", [E * CAP, ROW], F32).ap()

        frames = sb("frames", [FRAME, NT * R])
        dft = sb("dft", [FRAME, 2 * BINS])
        melT = sb("melT", [2 * BINS, MELS])
        dct = sb("dct_s", [MFCC, MELS])
        wtok = sb("wtok", [MFCC, D])
        tokw = sb("tokw", [MELS + 1, D])
        wlin = sb("wlin", [DC + 1, 2, 3 * D])
        taps = sb("taps", [128, 5, KW])
        tapb = sb("tapb", [128, 5])
        fwd = sb("fwd", [R, 3, FC])
        coef = sb("coef", [T, 3, FC])
        inv = sb("inv", [FC, 3, R])
        hfil = sb("hfil", [DC, 2, 2, T])
        hdec = sb("hdec", [DC, 2, T])
        alph = sb("alph", [DC, 2])
        winb = sb("winb", [DC, 2])
        bmat = sb("bmat", [1, 2, D])
        hT = sb("hT", [T, 2, D])
        habs = sb("habs", [T, 2])
        hrec = sb("hrec", [T, 2])
        hcoef = sb("hcoef", [FC, 2, 3, D])
        times = sb("times", [DC, T])
        wout = sb("wout", [DC + 1, 2, D])
        ident = sb("ident", [128, 128])
        identb = sb("identb", [128, 128], BF16)
        ln1 = sb("ln1", [DC, 2])
        ln2 = sb("ln2", [DC, 2])
        wqkv = sb("wqkv", [DC, 2, 3 * D])
        wo = sb("wo", [128, 2, D])
        kmask = sb("kmask", [128, HG * T])
        sel = sb("sel", [R, G, HG * T])
        vmask = sb("vmask", [HG * T, D])
        causal = sb("causal", [R, HG * T])
        causalb = sb("causalb", [R, HG * T], BF16)
        before = sb("before", [R, R])
        beforeb = sb("beforeb", [R, R], BF16)
        onesb = sb("onesb", [R, R], BF16)
        expert = sb("expert", [128, E])
        token = sb("token", [R, NT])
        wgate = sb("wgate", [DC, 2, E])
        wfc = sb("wfc", [DC, E, 2, FF])
        wpr = sb("wpr", [128, E, MC, D])
        epsc = sb("epsc", [128, 2])
        fill = sb("fill", [SR, SQ, ROW])

        def two(name, shape, dt=F32):
            x = sb(name, [shape[0], 2] + shape[1:], dt)
            return [x[:, p] for p in range(2)]

        early = ExitStack()
        late = sb

        def sb(name, shape, dt=F32):
            return early.enter_context(nc.sbuf_tensor(name, shape, dt))


        sq = two("sq", [2 * BINS, R])
        logmel = two("logmel", [64, R])
        h0a = sb("h0", [R, 3, D])
        h0 = [h0a[:, n] for n in range(3)]
        u = two("u", [R, D])
        uT = two("uT", [DC + 1, 2, R])
        z = two("z", [128, 5, G, T + KW - 1])
        y = two("y", [128, 5, R])
        early.close()
        sb = late
        hid = two("hid", [128, MC, CAP])
        ex = two("ex", [R, 2, D])
        nmax = two("nmax", [R, 2])
        ssum = two("ssum", [R, 2])
        rsum = two("rsum", [R, 2])
        v = two("v", [R, D])
        prod = sb("prod", [FC, 3, D])
        gate = sb("gate", [R, D])
        vT = two("vT", [DC + 1, 2, R])
        hv = sb("hv", [R, D])
        h1 = two("h1", [R, D])
        xp = two("xp", [R, D])
        an = two("an", [R, D])
        stat = sb("stat", [R, 3, 6])
        mv = sb("mv", [R, 3, 2])
        lnv = sb("lnv", [R, 4])
        rstd = sb("rstd", [R, 4])
        var2 = sb("var2", [R, 1])
        aT = two("aT", [DC, 2, R])
        qpad = sb("qpad", [128, 2, G * (R + T)])
        kx = sb("kx", [128, 2, G, HG * T])
        vt = sb("vt", [R, D])
        vx = sb("vx", [HG * T, G, D])
        smax = sb("smax", [R, HEADS])
        sc = sb("sc", [R, HEADS, T])
        es = sb("es", [R, HEADS, T])
        psm = sb("psm", [R, HEADS])
        prc = sb("prc", [R, HEADS])
        pn = sb("pn", [R, HEADS, T])
        pT = sb("pT", [HG * T, NG, R])
        yT = sb("yT", [128, 2, R])
        h2 = two("h2", [R, D])
        base = two("base", [R, D])
        xl = two("xl", [R, ROW])
        xlT = sb("xlT", [DC, 2, R])
        top = two("top", [R, 8])
        topi = two("topi", [R, 8], U32)
        ef = two("ef", [R, 2])
        diff = sb("diff", [R, 1])
        ed = sb("ed", [R, 1])
        den = sb("den", [R, 1])
        oh = sb("oh", [R, 2, E])
        chosen = two("chosen", [R, E], BF16)
        total = two("total", [R, E], BF16)
        junk = sb("junk", [R, 2, E])
        slot = sb("slot", [R, 2])
        over = sb("over", [R, 2])
        at = sb("at", [R, 2])
        atu = two("atu", [R, 2], U32)
        xe = two("xe", [SR, SQ, ROW])
        xeT = two("xeT", [DC, 2, CAP])
        ye = two("ye", [SR, SQ, D])
        first = sb("first", [SR, SQ])
        wa = sb("wa", [SR, SQ])
        wb = sb("wb", [SR, SQ])
        wt = two("wt", [SR, SQ])
        tok = two("tok", [SR, SQ], U32)

        PB = [ctx.enter_context(nc.psum_tensor(f"bank{i}", [128, 512], F32)) for i in range(8)]
        pspec, pmel, ptok = PB[0][0:2 * BINS, 0:R], PB[0][0:MELS, 0:R], PB[0][0:R, 0:D]
        puT = PB[0][0:DC, 0:2 * R].rearrange("p (c n) -> p c n", c=2)
        pz = PB[1][:, 0:4 * R].rearrange("p (c n) -> p c n", c=4)
        px = PB[1][0:R, 0:2 * D]
        pz4 = PB[2][0:64, 0:R]
        pv = PB[2][0:R, 0:D]
        pf01, pf2, py = PB[3][0:FC, 0:2 * D], PB[4][0:FC, 0:D], PB[4][0:R, 0:D]
        pvT = PB[3][0:DC, 0:2 * R].rearrange("p (c n) -> p c n", c=2)
        po = PB[4][0:R, 0:D]
        paT = PB[5][0:DC, 0:2 * R].rearrange("p (c n) -> p c n", c=2)
        pq = PB[5][:, 0:2 * R].rearrange("p (c n) -> p c n", c=2)
        pvv = PB[5][0:R, 256:256 + D]
        pk = PB[6][:, 0:2 * R].rearrange("p (c n) -> p c n", c=2)
        ps1 = PB[5][0:R, 0:HG * T].rearrange("p (h k) -> p h k", k=T)
        ps02 = PB[6][0:R, 0:2 * HG * T].rearrange("p (h k) -> p h k", k=T)
        ppT = PB[5][0:HG * T, 0:NG * R].rearrange("p (g n) -> p g n", g=NG)
        pvx = PB[7][0:HG * T, 0:2 * D].rearrange("p (b d) -> p b d", b=2)
        pyT = PB[7][:, 0:2 * R].rearrange("p (c n) -> p c n", c=2)
        pao = PB[7][0:R, 0:D]
        pxT = PB[2][0:DC, 0:2 * R].rearrange("p (c n) -> p c n", c=2)
        pg, ppos = PB[2][0:R, 0:E], PB[2][0:R, 0:E]

        for name in ("in_tok", "in_lin", "in_hyena", "in_ffn", "in_fill", "in_exp", "filled", "stored0", "stored1", "scattered0", "scattered1",
                     "in_slots0", "in_slots1", "added", "zeroed", "bf",
                     "dctw", "tokw", "dec", "decb", "fil", "filT", "habs", "hrec", "hT", "hc", "hcoef", "hb",
                     "spec", "sq", "mel", "logmel", "tok", "h0", "st0", "var0", "lnv0", "r0", "u", "uT", "uTs",
                     "z", "zs", "c1", "c2", "conv", "xT", "vT0", "nmax", "ex", "rsum", "v0",
                     "f0", "f1", "prod0", "prod1", "y0", "y1", "g0", "g1", "v1", "v2",
                     "vT", "vTs", "o", "hv", "h1", "st1", "var1", "lnv1", "r1", "xp", "var2", "lnv2", "r2", "an",
                     "aT", "aTs", "k", "qv", "qs", "vs", "kx", "vx0", "vx1", "vx2", "vxs0", "vxs1", "vxs2",
                     "s", "smax", "sc", "es", "psm", "prc", "pn", "pT", "pTs", "yT", "yTs", "ao", "h2", "base",
                     "st2", "var3", "lnv3", "r3", "xl", "xlT", "xlTs", "g", "top", "topi", "diff", "ed", "den",
                     "w0", "meta", "ef", "oh", "chosen", "total", "pos", "slot", "over", "at", "atu",
                     "xeT", "xeTs", "fc", "hid", "pr", "ye", "wfirst", "wab", "wt", "tki"):
            sem(name)

        def need(eng, name, value):
            if value > 0:
                eng.wait_ge(S[name], value)

        def lanes(j):
            return j, j - 1, j - 2, j - 3, j - 4, j - 5

        def ok(i):
            return 0 <= i < NT

        block = ctx.enter_context(nc.Block())

        @block.sync
        def _(sp):
            def load(dst, src, name):
                sp.dma_start(dst, src).then_inc(S[name], 16)

            load(dft[:], a["dft"], "in_tok")
            load(melT[:], a["melT"], "in_tok")
            load(dct[:], a["dct"], "in_tok")
            load(wtok[:], a["w_proj"], "in_tok")
            load(tokw[MELS:MELS + 1, :], a["b_proj"], "in_tok")
            load(frames[:], a["frames"], "in_tok")
            load(ident[:], a["ident"], "in_lin")
            load(wlin[:], a["wlin"], "in_lin")
            load(taps[:], a["taps"], "in_lin")
            load(tapb[:], a["tapb"], "in_lin")
            for dst, src in ((hfil, "hfil"), (alph, "alph"), (winb, "winb"), (bmat, "bmat"), (times, "time"),
                             (coef, "coef"), (fwd, "fwd"), (inv, "inv"), (wout, "wout")):
                load(dst[:], a[src], "in_hyena")
            for dst, src in ((ln1, "ln1"), (ln2, "ln2"), (wqkv, "wqkv"), (wo, "wo"), (kmask, "kmask"), (sel, "sel"),
                             (vmask, "vmask"), (causal, "causal"), (before, "before"), (expert, "expert"),
                             (token, "token"), (wgate, "wgate")):
                load(dst[:], a[src], "in_ffn")
            need(sp, "zeroed", 3)
            for e in range(E):
                sp.dma_start(slots[e * CAP:(e + 1) * CAP, :].rearrange("(q p) c -> p q c", p=SR), fill[:])\
                    .then_inc(S["filled"], 16)
            for e in range(E):
                load(wfc[:, e], a["c_fc"][e].rearrange("(k p) f -> p k f", p=DC), "in_exp")
                load(wpr[:, e], a["c_proj_e"][e].rearrange("(m p) d -> p m d", p=128), "in_exp")
            for i in range(NT):
                rows = R if i < NT - 1 else LAST
                need(sp, "base", i + 1)
                sp.dma_start(out[i * R:i * R + rows, :], base[i % 2][0:rows, :]).then_inc(S[f"stored{i % 2}"], 16)
            for p in range(2):
                sp.wait_ge(S[f"scattered{p}"], 16 * TOPK * ((NT + 1 - p) // 2))
            for e in range(E):
                if e >= 2:
                    sp.wait_ge(S["wt"], e - 1)
                    sp.wait_ge(S["xeT"], e - 1)
                    sp.wait_ge(S["tki"], e - 1)
                sp.dma_start(xe[e % 2], slots[e * CAP:(e + 1) * CAP, :].rearrange("(q p) c -> p q c", p=SR))\
                    .then_inc(S[f"in_slots{e % 2}"], 16)
            sp.wait_ge(S["added"], 16 * SQ * E)

        @block.tensor
        def _(pe):
            mm, tr = pe.matmul, pe.transpose

            pe.wait_ge(S["in_tok"], 16 * 6)
            mm(PB[0][0:MELS, 0:D], dct[:], wtok[:], start=True, stop=True).then_inc(S["dctw"], 1)
            pe.wait_ge(S["zeroed"], 3)
            pe.wait_ge(S["tokw"], 1)

            def a_spec(i):
                need(pe, "uTs", i)
                mm(pspec, dft[:], frames[:, i * R:(i + 1) * R], start=True, stop=True).then_inc(S["spec"], 1)

            def a_mel(i):
                pe.wait_ge(S["sq"], i + 1)
                mm(pmel, melT[:], sq[i % 2], start=True, stop=True).then_inc(S["mel"], 1)

            def a_tok(i):
                pe.wait_ge(S["logmel"], i + 1)
                mm(ptok, logmel[i % 2][0:MELS + 1, :], tokw[:], start=True, stop=True).then_inc(S["tok"], 1)

            def a_uT(i):
                if i == 0:
                    pe.wait_ge(S["in_lin"], 16 * 4)
                pe.wait_ge(S["u"], i + 1)
                for k in range(2):
                    last = tr(puT[:, k], u[i % 2][:, k * DC:(k + 1) * DC], ident[0:R, 0:R])
                last.then_inc(S["uT"], 1)

            def a_z(i):
                need(pe, "ex", i)
                need(pe, "v0", i)
                need(pe, "topi", i - 3)
                pe.wait_ge(S["uTs"], i + 1)
                for c, m in enumerate(ZC):
                    dst = pz[:, c] if c < 4 else pz4
                    for k in range(2):
                        kk = DC + k
                        last = mm(dst, wlin[0:kk, k, c * 128:c * 128 + m], uT[i % 2][0:kk, k],
                                  start=k == 0, stop=k == 1)
                last.then_inc(S["z"], 1)

            def a_xT(i):
                pe.wait_ge(S["conv"], i + 1)
                for c in range(3):
                    last = tr(px[:, c * 128:(c + 1) * 128], y[i % 2][:, c], ident[:])
                last.then_inc(S["xT"], 1)
                need(pe, "slot", i - 3)
                tr(pv[:, 0:128], y[i % 2][:, 3], ident[:])
                tr(pv[:, 128:192], y[i % 2][0:64, 4], ident[0:64, 0:64]).then_inc(S["vT0"], 1)

            def b_f(i, o):
                if i == 0 and o == 0:
                    pe.wait_ge(S["in_hyena"], 16 * 9)
                if o == 0:
                    need(pe, "vTs", i)
                    need(pe, "h1", i)
                pe.wait_ge(S[f"v{o}"], i + 1)
                for c in range(3):
                    last = mm(pf01[:, c * D:(c + 1) * D] if c < 2 else pf2, fwd[:, c], v[i % 2],
                              start=True, stop=True)
                last.then_inc(S[f"f{o}"], 1)

            def b_y(i, o):
                pe.wait_ge(S[f"prod{o}"], i + 1)
                for c in range(3):
                    last = mm(py, inv[:, c], prod[:, c], start=c == 0, stop=c == 2)
                last.then_inc(S[f"y{o}"], 1)

            def b_vT(i):
                pe.wait_ge(S["v2"], i + 1)
                for k in range(2):
                    last = tr(pvT[:, k], v[i % 2][:, k * DC:(k + 1) * DC], ident[0:R, 0:R])
                last.then_inc(S["vT"], 1)

            def b_o(i):
                pe.wait_ge(S["vTs"], i + 1)
                for k in range(2):
                    last = mm(po, vT[i % 2][0:DC + k, k], wout[0:DC + k, k], start=k == 0, stop=k == 1)
                last.then_inc(S["o"], 1)

            def c_aT(i):
                if i == 0:
                    pe.wait_ge(S["in_ffn"], 16 * 12)
                need(pe, "pTs", i)
                pe.wait_ge(S["an"], i + 1)
                for k in range(2):
                    last = tr(paT[:, k], an[i % 2][:, k * DC:(k + 1) * DC], ident[0:R, 0:R])
                last.then_inc(S["aT"], 1)

            def c_qkv(i):
                pe.wait_ge(S["aTs"], i + 1)
                need(pe, "sc", i)
                for n, dst in ((1, pk), (0, pq)):
                    for c, m in ((0, 128), (1, 64)):
                        for k in range(2):
                            last = mm(dst[0:m, c], wqkv[:, k, n * D + c * 128:n * D + c * 128 + m], aT[i % 2][:, k],
                                      start=k == 0, stop=k == 1)
                    if n:
                        last.then_inc(S["k"], 1)
                for k in range(2):
                    last = mm(pvv, aT[i % 2][:, k], wqkv[:, k, 2 * D:], start=k == 0, stop=k == 1)
                last.then_inc(S["qv"], 1)

            def c_vx(i, n):
                if n == 0:
                    need(pe, "h2", i)
                    pe.wait_ge(S["vs"], i + 1)
                else:
                    pe.wait_ge(S[f"vxs{n - 1}"], i + 1)
                for b in range(2 * n, min(2 * n + 2, G)):
                    last = mm(pvx[:, b - 2 * n], sel[:, b], vt[:], start=True, stop=True)
                last.then_inc(S[f"vx{n}"], 1)

            def c_s(i):
                if i == 0:
                    pe.wait_ge(S["bf"], 2)
                pe.wait_ge(S["qs"], i + 1)
                pe.wait_ge(S["kx"], i + 1)
                for g, dst, r0, c in ((0, ps02[:, 0:HG], 0, 0), (1, ps1, 64, 0), (2, ps02[:, HG:2 * HG], 0, 1)):
                    mm(dst, identb[0:R, 0:R], causalb[:], start=True, stop=False)
                    for b in range(G):
                        last = mm(dst, qpad[r0:r0 + GD, c, b * R:(b + 1) * R], kx[r0:r0 + GD, c, b], start=False, stop=b == G - 1)
                last.then_inc(S["s"], 1)

            def c_pT(i):
                pe.wait_ge(S["pn"], i + 1)
                for g in range(NG):
                    last = tr(ppT[:, g], pn[:, g * HG:(g + 1) * HG], ident[0:R, 0:R])
                last.then_inc(S["pT"], 1)

            def c_yT(i):
                pe.wait_ge(S["pTs"], i + 1)
                pe.wait_ge(S["vxs2"], i + 1)
                for g in range(NG):
                    r0 = GD * (g % 2)
                    for b in range(G):
                        last = mm(pyT[r0:r0 + GD, g // 2, b * T:(b + 1) * T], vx[:, b, g * GD:(g + 1) * GD],
                                  pT[:, g, b * T:(b + 1) * T], start=True, stop=True)
                last.then_inc(S["yT"], 1)

            def c_ao(i):
                pe.wait_ge(S["yTs"], i + 1)
                mm(pao, yT[:, 0], wo[:, 0], start=True, stop=False)
                mm(pao, yT[0:64, 1], wo[0:64, 1], start=False, stop=True).then_inc(S["ao"], 1)

            def c_xlT(i):
                need(pe, "v0", min(i + 4, NT))
                pe.wait_ge(S["xl"], i + 1)
                for k in range(2):
                    last = tr(pxT[:, k], xl[i % 2][:, k * DC:(k + 1) * DC], ident[0:R, 0:R])
                last.then_inc(S["xlT"], 1)

            def c_gate(i):
                pe.wait_ge(S["xlTs"], i + 1)
                for k in range(2):
                    last = mm(pg, xlT[:, k], wgate[:, k], start=k == 0, stop=k == 1)
                last.then_inc(S["g"], 1)

            def c_pos(i):
                need(pe, "zs", min(i + 5, NT))
                pe.wait_ge(S["topi"], i + 1)
                pe.wait_ge(S["chosen"], i + 1)
                need(pe, "total", i)
                last = mm(ppos, beforeb[:], chosen[i % 2], start=True, stop=i == 0)
                if i:
                    last = mm(ppos, onesb[:], total[(i - 1) % 2], start=False, stop=True)
                last.then_inc(S["pos"], 1)

            def filters():
                pe.wait_ge(S["fil"], 2)
                for o in range(2):
                    for k in range(2):
                        last = tr(PB[7][0:T, o * D + k * DC:o * D + (k + 1) * DC], hfil[:, o, k], ident[0:DC, 0:DC])
                last.then_inc(S["filT"], 1)
                pe.wait_ge(S["hT"], 2)
                pe.wait_ge(S["hb"], 1)
                for o in range(2):
                    if o:
                        pe.wait_ge(S["hcoef"], 1)
                    for c in range(3):
                        last = mm((pf01[:, c * D:(c + 1) * D] if c < 2 else pf2), coef[:, c], hT[:, o],
                                  start=True, stop=True)
                    last.then_inc(S["hc"], 1)
                pe.wait_ge(S["hcoef"], 2)

            for j in range(NT + LANES - 1):
                t, i, b, c, k, d = lanes(j)
                if ok(d): c_xlT(d)
                if ok(b): b_f(b, 0)
                if ok(i): a_uT(i)
                if ok(k): c_pT(k)
                if ok(d): c_gate(d)
                if ok(i): a_z(i)
                if ok(c): c_aT(c)
                if ok(k): c_yT(k)
                if ok(b): b_y(b, 0)
                if ok(d): c_pos(d)
                if ok(c): c_qkv(c)
                if ok(k): c_ao(k)
                if ok(b): b_f(b, 1)
                if ok(t): a_spec(t)
                if ok(c): c_vx(c, 0)
                if ok(t): a_mel(t)
                if ok(b): b_y(b, 1)
                if ok(c): c_s(c)
                if ok(b): b_vT(b)
                if ok(c): c_vx(c, 1)
                if ok(t): a_tok(t)
                if ok(i): a_xT(i)
                if ok(b): b_o(b)
                if ok(c): c_vx(c, 2)
                if j == 0: filters()

            def e_xT(e):
                need(pe, "xeTs", e)
                pe.wait_ge(S[f"in_slots{e % 2}"], 16 * (e // 2 + 1))
                for k in range(2):
                    for q in range(SQ):
                        last = tr(PB[k][0:DC, q * SR:(q + 1) * SR], xe[e % 2][:, q, k * DC:(k + 1) * DC],
                                  ident[0:SR, 0:SR])
                last.then_inc(S["xeT"], 1)

            def e_fc(e):
                pe.wait_ge(S["xeTs"], e + 1)
                for m in range(MC):
                    n = e * MC + m
                    need(pe, "hid", n - 3)
                    for k in range(2):
                        last = mm(PB[2 + n % 4][:, 0:CAP], wfc[:, e, k, m * 128:(m + 1) * 128], xeT[e % 2][:, k],
                                  start=k == 0, stop=k == 1)
                    last.then_inc(S["fc"], 1)

            def e_pr(e):
                for q in range(SQ):
                    if q % 2 == 0:
                        need(pe, "ye", SQ * (e - 1) + q + 2)
                    for m in range(MC):
                        if q == 0:
                            pe.wait_ge(S["hid"], e * MC + m + 1)
                        last = mm(PB[6 + q // 2][0:SR, (q % 2) * D:(q % 2 + 1) * D],
                                  hid[e % 2][:, m, q * SR:(q + 1) * SR], wpr[:, e, m], start=m == 0, stop=m == MC - 1)
                    last.then_inc(S["pr"], 1)

            pe.wait_ge(S["in_exp"], 16 * 2 * E)
            pe.wait_ge(S["slot"], NT)
            e_xT(0)
            for e in range(E):
                e_fc(e)
                if e + 1 < E:
                    e_xT(e + 1)
                e_pr(e)

        @block.scalar
        def _(act):
            f = act.activation

            def rstd_of(name, n, src, i):
                act.wait_ge(S[{0: "var0", 1: "var1", 2: "var2", 3: "var3"}[n]], i + 1)
                f(lnv[:, n:n + 1], src, ACT.Ln, bias=epsc[0:R, 0:1]).then_inc(S[f"lnv{n}"], 1)
                act.wait_ge(S[f"lnv{n}"], i + 1)
                f(rstd[:, n:n + 1], lnv[:, n:n + 1], ACT.Exp, scale=-0.5).then_inc(S[f"r{n}"], 1)

            act.preload_act_table_set("natural_log_exp_and_others")
            act.wait_ge(S["zeroed"], 3)
            act.wait_ge(S["dctw"], 1)
            f(tokw[0:MELS, :], PB[0][0:MELS, 0:D], ACT.Copy).then_inc(S["tokw"], 1)

            def a_sq(i):
                act.wait_ge(S["spec"], i + 1)
                need(act, "mel", i - 1)
                f(sq[i % 2], pspec, ACT.Square).then_inc(S["sq"], 1)

            def a_log(i):
                act.wait_ge(S["mel"], i + 1)
                need(act, "tok", i - 1)
                f(logmel[i % 2][0:MELS, :], pmel, ACT.Ln, bias=epsc[0:MELS, 1:2]).then_inc(S["logmel"], 1)

            def a_h0(i):
                act.wait_ge(S["tok"], i + 1)
                need(act, "hv", i - 2)
                f(h0[i % 3], ptok, ACT.Copy).then_inc(S["h0"], 1)

            def a_r(i):
                rstd_of("0", 0, mv[:, 0, 1:2], i)

            def a_uTs(i):
                act.wait_ge(S["uT"], i + 1)
                need(act, "z", i - 1)
                f(uT[i % 2][0:DC], puT, ACT.Copy).then_inc(S["uTs"], 1)

            def a_zs(i):
                act.wait_ge(S["z"], i + 1)
                need(act, "conv", i - 1)
                f(z[i % 2][:, 0:4].rearrange("p c b t -> p (c b) t")[:, :, KW - 1:],
                  pz.rearrange("p c (b t) -> p (c b) t", t=T), ACT.Copy)
                f(z[i % 2][0:64, 4, :, KW - 1:], pz4.rearrange("p (b t) -> p b t", t=T), ACT.Copy)\
                    .then_inc(S["zs"], 1)

            def a_ex(i):
                act.wait_ge(S["nmax"], i + 1)
                need(act, "g1", i - 1)
                need(act, "rsum", i - 1)
                for o in range(2):
                    last = f(ex[i % 2][:, o], px[:, o * D:(o + 1) * D], ACT.Exp, bias=nmax[i % 2][:, o:o + 1],
                             accum_out=ssum[i % 2][:, o:o + 1])
                last.then_inc(S["ex"], 1)

            def b_vTs(i):
                act.wait_ge(S["vT"], i + 1)
                need(act, "o", i - 1)
                f(vT[i % 2][0:DC], pvT, ACT.Copy).then_inc(S["vTs"], 1)

            def b_r(i):
                rstd_of("1", 1, mv[:, 1, 1:2], i)

            def b_r2(i):
                rstd_of("2", 2, var2[:], i)

            def c_aTs(i):
                if i == 0:
                    act.wait_ge(S["in_ffn"], 16 * 12)
                act.wait_ge(S["aT"], i + 1)
                need(act, "qv", i - 1)
                for k in range(2):
                    last = f(aT[i % 2][:, k], paT[:, k], ACT.Copy, scale=ln1[:, k:k + 1])
                last.then_inc(S["aTs"], 1)

            def c_qs(i):
                act.wait_ge(S["qv"], i + 1)
                need(act, "s", i)
                for c, m in ((0, 128), (1, 64)):
                    own = qpad[0:m, c].rearrange("p (b n) -> p b n", b=G)[:, :, 0:T]
                    last = f(own, pq[0:m, c].rearrange("p (b t) -> p b t", t=T), ACT.Copy)
                last.then_inc(S["qs"], 1)

            def c_vs(i):
                act.wait_ge(S["qv"], i + 1)
                need(act, "vx2", i)
                f(vt[:], pvv, ACT.Copy).then_inc(S["vs"], 1)

            def c_es(i):
                act.wait_ge(S["sc"], i + 1)
                need(act, "pn", i)
                f(es[:], sc[:], ACT.Exp, scale=SCALE).then_inc(S["es"], 1)

            def c_pTs(i):
                act.wait_ge(S["pT"], i + 1)
                need(act, "yT", i)
                f(pT[:], ppT, ACT.Copy).then_inc(S["pTs"], 1)

            def c_yTs(i):
                act.wait_ge(S["yT"], i + 1)
                need(act, "ao", i)
                f(yT[:, 0], pyT[:, 0], ACT.Copy)
                f(yT[0:64, 1], pyT[0:64, 1], ACT.Copy).then_inc(S["yTs"], 1)

            def c_r(i):
                rstd_of("3", 3, mv[:, 2, 1:2], i)

            def c_xlTs(i):
                act.wait_ge(S["xlT"], i + 1)
                need(act, "g", i)
                for k in range(2):
                    last = f(xlT[:, k], pxT[:, k], ACT.Copy, scale=ln2[:, k:k + 1])
                last.then_inc(S["xlTs"], 1)

            def c_ed(i):
                act.wait_ge(S["diff"], i + 1)
                need(act, "w0", i)
                f(ed[:], diff[:], ACT.Exp).then_inc(S["ed"], 1)

            def filters():
                act.wait_ge(S["in_hyena"], 16 * 9)
                for k in range(2):
                    last = f(hdec[:, k], times[:], ACT.Exp, scale=alph[:, k:k + 1])
                last.then_inc(S["dec"], 1)

            for j in range(NT + LANES - 1):
                t, i, b, c, k, d = lanes(j)
                if j == 0: filters()
                if ok(c): b_r(c)
                if ok(d): c_xlTs(d)
                if ok(i): a_uTs(i)
                if ok(c): b_r2(c)
                if ok(k): c_pTs(k)
                if ok(i): a_zs(i)
                if ok(c): c_aTs(c)
                if ok(k): c_yTs(k)
                if ok(d): c_ed(d)
                if ok(c): c_vs(c)
                if ok(c): c_qs(c)
                if ok(t): a_sq(t)
                if ok(t): a_log(t)
                if ok(k): c_r(k)
                if ok(b): b_vTs(b)
                if ok(t): a_h0(t)
                if ok(c): c_es(c)
                if ok(t): a_r(t)
                if ok(i): a_ex(i)

            for e in range(E):
                for m in range(MC):
                    n = e * MC + m
                    act.wait_ge(S["fc"], n + 1)
                    if m == 0:
                        need(act, "pr", SQ * (e - 1))
                    f(hid[e % 2][:, m], PB[2 + n % 4][:, 0:CAP], ACT.Gelu).then_inc(S["hid"], 1)

        @block.vector
        def _(ve):
            tt, ts, stt = ve.tensor_tensor, ve.tensor_scalar, ve.scalar_tensor_tensor

            def layer_stats(n, src, i, var):
                ve.bn_stats(stat[:, n], src).then_inc(S[f"st{n}"], 1)
                ve.wait_ge(S[f"st{n}"], i + 1)
                ve.bn_aggr(mv[:, n], stat[:, n]).then_inc(S[var], 1)

            def a_stats(i):
                ve.wait_ge(S["h0"], i + 1)
                layer_stats(0, h0[i % 3], i, "var0")

            def a_u(i):
                ve.wait_ge(S["r0"], i + 1)
                need(ve, "uT", i - 1)
                ts(u[i % 2], h0[i % 3], mv[:, 0, 0:1], rstd[:, 0:1], ALU.subtract, ALU.mult).then_inc(S["u"], 1)

            def yv(i, c):
                return y[i % 2][0:ZC[c], c].rearrange("p (b t) -> p b t", t=T)

            def tap(i, k):
                for c in range(5):
                    zk = z[i % 2][0:ZC[c], c, :, k:k + T]
                    if k == 0:
                        last = ts(yv(i, c), zk, taps[0:ZC[c], c, 0:1], tapb[0:ZC[c], c:c + 1], ALU.mult, ALU.add)
                    else:
                        last = stt(yv(i, c), zk, taps[0:ZC[c], c, k:k + 1], yv(i, c), ALU.mult, ALU.add)
                return last

            def a_conv1(i):
                ve.wait_ge(S["zs"], i + 1)
                need(ve, "vT0", i - 1)
                tap(i, 0).then_inc(S["c1"], 1)

            def a_conv2(i):
                ve.wait_ge(S["c1"], i + 1)
                tap(i, 1).then_inc(S["c2"], 1)

            def a_conv3(i):
                ve.wait_ge(S["c2"], i + 1)
                tap(i, 2).then_inc(S["conv"], 1)

            def a_nmax(i):
                ve.wait_ge(S["xT"], i + 1)
                ve.tensor_reduce(nmax[i % 2], px.rearrange("p (o d) -> p o d", o=2), AX.X, ALU.max, negate=True)\
                    .then_inc(S["nmax"], 1)

            def a_v0(i):
                ve.wait_ge(S["vT0"], i + 1)
                need(ve, "vT", i - 1)
                need(ve, "hv", i - 1)
                tt(v[i % 2], pv, u[i % 2], ALU.add).then_inc(S["v0"], 1)

            def a_rsum(i):
                ve.wait_ge(S["ex"], i + 1)
                ve.reciprocal(rsum[i % 2], ssum[i % 2]).then_inc(S["rsum"], 1)

            def b_prod(i, o):
                ve.wait_ge(S[f"f{o}"], i + 1)
                if o == 1:
                    ve.wait_ge(S["y0"], i + 1)
                else:
                    need(ve, "y1", i)
                tt(prod[:, 0:2].rearrange("p c d -> p (c d)"), pf01,
                   hcoef[:, o, 0:2].rearrange("p c d -> p (c d)"), ALU.mult)
                tt(prod[:, 2], pf2, hcoef[:, o, 2], ALU.mult).then_inc(S[f"prod{o}"], 1)

            def b_v(i, o):
                ve.wait_ge(S[f"y{o}"], i + 1)
                ve.wait_ge(S["rsum"], i + 1)
                stt(gate[:], ex[i % 2][:, o], rsum[i % 2][:, o:o + 1], py, ALU.mult, ALU.mult)\
                    .then_inc(S[f"g{o}"], 1)
                ve.wait_ge(S[f"g{o}"], i + 1)
                tt(v[i % 2], v[i % 2], gate[:], ALU.add).then_inc(S[f"v{o + 1}"], 1)

            def b_h1(i):
                ve.wait_ge(S["o"], i + 1)
                ve.wait_ge(S["hv"], i + 1)
                need(ve, "base", i - 1)
                tt(h1[i % 2], po, hv[:], ALU.add).then_inc(S["h1"], 1)
                ve.wait_ge(S["h1"], i + 1)
                layer_stats(1, h1[i % 2], i, "var1")

            def b_xp(i):
                ve.wait_ge(S["r1"], i + 1)
                stt(var2[:], mv[:, 1, 1:2], rstd[:, 1:2], rstd[:, 1:2], ALU.mult, ALU.mult).then_inc(S["var2"], 1)
                ts(xp[i % 2], h1[i % 2], mv[:, 1, 0:1], rstd[:, 1:2], ALU.subtract, ALU.mult).then_inc(S["xp"], 1)

            def b_an(i):
                ve.wait_ge(S["xp"], i + 1)
                ve.wait_ge(S["r2"], i + 1)
                need(ve, "aT", i - 1)
                ts(an[i % 2], xp[i % 2], rstd[:, 2:3], None, ALU.mult).then_inc(S["an"], 1)

            def c_kx(i):
                if i == 0:
                    ve.wait_ge(S["in_ffn"], 16 * 12)
                ve.wait_ge(S["k"], i + 1)
                need(ve, "s", i)
                for c, m in ((0, 128), (1, 64)):
                    src = pk[0:m, c].rearrange("p (b k) -> p b k", k=T)[:, :, None, :].broadcast_to([m, G, HG, T])
                    msk = kmask[0:m].rearrange("p (h k) -> p h k", k=T)[:, None].broadcast_to([m, G, HG, T])
                    last = tt(kx[0:m, c].rearrange("p b (h k) -> p b h k", k=T), src, msk, ALU.mult)
                last.then_inc(S["kx"], 1)

            def c_vxs(i, n):
                if n == 0:
                    need(ve, "yT", i)
                ve.wait_ge(S[f"vx{n}"], i + 1)
                k = min(2, G - 2 * n)
                tt(vx[:, 2 * n:2 * n + k], pvx[:, 0:k], vmask[:, None, :].broadcast_to([HG * T, k, D]), ALU.mult)\
                    .then_inc(S[f"vxs{n}"], 1)

            SCORES = ((ps02[:, 0:HG], slice(0, HG)), (ps1, slice(HG, 2 * HG)), (ps02[:, HG:2 * HG], slice(2 * HG, 3 * HG)))

            def c_sc(i):
                ve.wait_ge(S["s"], i + 1)
                for src, hs in SCORES:
                    last = ve.tensor_reduce(smax[:, hs], src, AX.X, ALU.max)
                last.then_inc(S["smax"], 1)
                ve.wait_ge(S["smax"], i + 1)
                need(ve, "es", i)
                for src, hs in SCORES:
                    last = tt(sc[:, hs], src, smax[:, hs, None].broadcast_to([R, HG, T]), ALU.subtract)
                last.then_inc(S["sc"], 1)

            def c_pn(i):
                ve.wait_ge(S["es"], i + 1)
                ve.tensor_reduce(psm[:], es[:], AX.X, ALU.add).then_inc(S["psm"], 1)
                ve.wait_ge(S["psm"], i + 1)
                ve.reciprocal(prc[:], psm[:]).then_inc(S["prc"], 1)
                ve.wait_ge(S["prc"], i + 1)
                need(ve, "pT", i)
                tt(pn[:], es[:], prc[:, :, None].broadcast_to([R, HEADS, T]), ALU.mult).then_inc(S["pn"], 1)

            def c_h2(i):
                ve.wait_ge(S["ao"], i + 1)
                need(ve, "base", i - 1)
                tt(h2[i % 2], pao, xp[i % 2], ALU.add).then_inc(S["h2"], 1)
                ve.wait_ge(S["h2"], i + 1)
                layer_stats(2, h2[i % 2], i, "var3")

            def c_xl(i):
                ve.wait_ge(S["r3"], i + 1)
                if i >= 2:
                    ve.wait_ge(S[f"scattered{i % 2}"], 16 * TOPK * (i // 2))
                need(ve, "xlT", i - 1)
                ts(xl[i % 2][:, 0:D], h2[i % 2], mv[:, 2, 0:1], rstd[:, 3:4], ALU.subtract, ALU.mult)\
                    .then_inc(S["xl"], 1)

            def c_route(i):
                p = i % 2
                ve.wait_ge(S["g"], i + 1)
                ve.max(top[p], pg).then_inc(S["top"], 1)
                ve.wait_ge(S["top"], i + 1)
                ve.max_index(topi[p], top[p], pg).then_inc(S["topi"], 1)
                tt(diff[:], top[p][:, 1:2], top[p][:, 0:1], ALU.subtract).then_inc(S["diff"], 1)
                ve.wait_ge(S["topi"], i + 1)
                ve.tensor_copy(ef[p], topi[p][:, 0:2]).then_inc(S["ef"], 1)
                ve.wait_ge(S["ef"], i + 1)
                for k in range(2):
                    last = ts(oh[:, k], expert[0:R], ef[p][:, k:k + 1], None, ALU.is_equal)
                last.then_inc(S["oh"], 1)
                ve.wait_ge(S["oh"], i + 1)
                need(ve, "pos", i - 1)
                tt(chosen[p], oh[:, 0], oh[:, 1], ALU.add).then_inc(S["chosen"], 1)
                ve.wait_ge(S["chosen"], i + 1)
                if i == 0:
                    ve.tensor_copy(total[0], chosen[0]).then_inc(S["total"], 1)
                else:
                    tt(total[p], total[1 - p], chosen[p], ALU.add).then_inc(S["total"], 1)

            def c_slots(i):
                p = i % 2
                ve.wait_ge(S["ed"], i + 1)
                ts(den[:], ed[:], 1.0, None, ALU.add).then_inc(S["den"], 1)
                ve.wait_ge(S["den"], i + 1)
                ve.reciprocal(xl[p][:, D + 2:D + 3], den[:]).then_inc(S["w0"], 1)
                ve.wait_ge(S["w0"], i + 1)
                tt(xl[p][:, D + 3:D + 4], ed[:], xl[p][:, D + 2:D + 3], ALU.mult)
                ve.tensor_copy(xl[p][:, D + 1:D + 2], ef[p][:, 0:1])
                ve.tensor_copy(xl[p][:, D:D + 1], token[:, i:i + 1]).then_inc(S["meta"], 1)
                ve.wait_ge(S["pos"], i + 1)
                for k in range(2):
                    last = ve.tensor_tensor_reduce(junk[:, k], ppos, oh[:, k], 1.0, 0.0, ALU.mult, ALU.add,
                                                   slot[:, k:k + 1])
                last.then_inc(S["slot"], 1)
                ve.wait_ge(S["slot"], i + 1)
                ts(over[:], slot[:], float(CAP), NOWHERE, ALU.is_ge, ALU.mult).then_inc(S["over"], 1)
                stt(at[:], ef[p], float(CAP), slot[:], ALU.mult, ALU.add)
                ve.wait_ge(S["over"], i + 1)
                tt(slot[:], over[:], slot[:], ALU.add).then_inc(S["at"], 1)
                ve.wait_ge(S["at"], i + 1)
                stt(atu[p], ef[p], float(CAP), slot[:], ALU.mult, ALU.add).then_inc(S["atu"], 1)

            ve.memset(epsc[:, 0:1], EPS)
            ve.memset(epsc[:, 1:2], 1e-6)
            for p in range(2):
                ve.memset(logmel[p], 1.0)
                ve.memset(uT[p], 1.0)
                ve.memset(vT[p], 1.0)
                ve.memset(z[p], 0.0)
            ve.memset(qpad[:], 0.0)
            ve.memset(onesb[:], 1.0).then_inc(S["zeroed"], 1)
            ve.memset(fill[:], 0.0).then_inc(S["zeroed"], 1)
            ve.wait_ge(S["zeroed"], 2)
            ve.memset(fill[:, :, D:D + 1], NOWHERE).then_inc(S["zeroed"], 1)

            def filters():
                ve.wait_ge(S["dec"], 1)
                for k in range(2):
                    last = ts(hdec[:, k], hdec[:, k], winb[:, k:k + 1], None, ALU.add)
                last.then_inc(S["decb"], 1)
                ve.wait_ge(S["decb"], 1)
                for o in range(2):
                    tt(hfil[:, o], hfil[:, o], hdec[:], ALU.mult).then_inc(S["fil"], 1)
                ve.wait_ge(S["filT"], 1)
                src = PB[7][0:T, 0:2 * D].rearrange("p (o d) -> p o d", o=2)
                ve.tensor_reduce(habs[:], src, AX.X, ALU.add, apply_absolute_value=True).then_inc(S["habs"], 1)
                ve.wait_ge(S["habs"], 1)
                ve.reciprocal(hrec[:], habs[:]).then_inc(S["hrec"], 1)
                ve.wait_ge(S["hrec"], 1)
                for o in range(2):
                    ts(hT[:, o], src[:, o], hrec[:, o:o + 1], None, ALU.mult).then_inc(S["hT"], 1)
                ve.wait_ge(S["hT"], 2)
                tt(hT[0:1], hT[0:1], bmat[:], ALU.add).then_inc(S["hb"], 1)
                for o in range(2):
                    ve.wait_ge(S["hc"], o + 1)
                    ve.tensor_copy(hcoef[:, o, 0:2].rearrange("p c d -> p (c d)"), pf01)
                    ve.tensor_copy(hcoef[:, o, 2], pf2).then_inc(S["hcoef"], 1)

            for j in range(NT + LANES - 1):
                t, i, b, c, k, d = lanes(j)
                if ok(b): b_prod(b, 0)
                if ok(d): c_route(d)
                if ok(c): b_xp(c)
                if ok(c): b_an(c)
                if ok(b): a_rsum(b)
                if ok(i): a_conv1(i)
                if ok(b): b_v(b, 0)
                if ok(d): c_slots(d)
                if ok(c): c_kx(c)
                if ok(i): a_conv2(i)
                if ok(b): b_prod(b, 1)
                if ok(k): c_h2(k)
                if ok(c): c_vxs(c, 0)
                if ok(b): b_v(b, 1)
                if ok(i): a_conv3(i)
                if ok(c): c_sc(c)
                if ok(k): c_xl(k)
                if ok(c): c_vxs(c, 1)
                if ok(t): a_stats(t)
                if ok(i): a_v0(i)
                if ok(i): a_nmax(i)
                if ok(c): c_pn(c)
                if ok(b): b_h1(b)
                if ok(c): c_vxs(c, 2)
                if ok(t): a_u(t)
                if j == 0:
                    filters()
                    ve.wait_ge(S["in_ffn"], 16 * 12)
                    ve.tensor_copy(causalb[:], causal[:])
                    ve.tensor_copy(beforeb[:], before[:]).then_inc(S["bf"], 1)
                    ve.wait_ge(S["in_lin"], 16 * 4)
                    ve.tensor_copy(identb[:], ident[:]).then_inc(S["bf"], 1)

            def e_xTs(e):
                ve.wait_ge(S["xeT"], e + 1)
                need(ve, "fc", MC * (e - 1))
                for k in range(2):
                    last = ts(xeT[e % 2][:, k], PB[k][0:DC, 0:CAP], ln2[:, k:k + 1], None, ALU.mult)
                last.then_inc(S["xeTs"], 1)

            def e_meta(e):
                x = xe[e % 2]
                ve.wait_ge(S[f"in_slots{e % 2}"], 16 * (e // 2 + 1))
                if e >= 2:
                    ve.wait_ge(S["added"], 16 * SQ * (e - 1))
                ve.tensor_copy(tok[e % 2], x[:, :, D]).then_inc(S["tki"], 1)
                ts(first[:], x[:, :, D + 1], float(e), None, ALU.is_equal).then_inc(S["wfirst"], 1)
                ve.wait_ge(S["wfirst"], e + 1)
                tt(wa[:], first[:], x[:, :, D + 2], ALU.mult)
                stt(wb[:], first[:], 0.0, x[:, :, D + 3], ALU.is_equal, ALU.mult).then_inc(S["wab"], 1)
                ve.wait_ge(S["wab"], e + 1)
                tt(wt[e % 2], wa[:], wb[:], ALU.add).then_inc(S["wt"], 1)

            e_xTs(0)
            e_meta(0)
            for e in range(E):
                if e + 1 < E:
                    e_xTs(e + 1)
                    e_meta(e + 1)
                ve.wait_ge(S["wt"], e + 1)
                if e >= 2:
                    ve.wait_ge(S["added"], 16 * SQ * (e - 1))
                for q in range(SQ):
                    ve.wait_ge(S["pr"], SQ * e + q // 2 * 2 + 2)
                    ts(ye[e % 2][:, q], PB[6 + q // 2][0:SR, (q % 2) * D:(q % 2 + 1) * D], wt[e % 2][:, q:q + 1],
                       None, ALU.mult).then_inc(S["ye"], 1)

        @block.gpsimd
        def _(pool):
            def b_hv(i):
                pool.wait_ge(S["v2"], i + 1)
                pool.wait_ge(S["h0"], i + 1)
                need(pool, "h1", i)
                pool.tensor_tensor(hv[:], v[i % 2], h0[i % 3], ALU.add).then_inc(S["hv"], 1)

            def c_base(i):
                pool.wait_ge(S["h2"], i + 1)
                pool.wait_ge(S["h1"], i + 1)
                if i >= 2:
                    pool.wait_ge(S[f"stored{i % 2}"], 16 * (i // 2))
                pool.tensor_tensor(base[i % 2], h2[i % 2], h1[i % 2], ALU.add).then_inc(S["base"], 1)

            def c_scatter(i):
                rows = R if i < NT - 1 else LAST
                if i == 0:
                    pool.wait_ge(S["filled"], 16 * E)
                pool.wait_ge(S["meta"], i + 1)
                pool.wait_ge(S["atu"], i + 1)
                for k in range(TOPK):
                    pool.indirect_dma_start(
                        slots, bass.IndirectOffsetOnAxis(ap=atu[i % 2][0:rows, k:k + 1], axis=0),
                        xl[i % 2][0:rows, :], None, bounds_check=E * CAP - 1, oob_is_err=False)\
                        .then_inc(S[f"scattered{i % 2}"], 16)

            for j in range(NT + LANES - 1):
                t, i, b, c, k, d = lanes(j)
                if ok(d): c_scatter(d)
                if ok(k): c_base(k)
                if ok(b): b_hv(b)

            for p in range(2):
                pool.wait_ge(S[f"stored{p}"], 16 * ((NT + 1 - p) // 2))
            for e in range(E):
                if e:
                    pool.wait_ge(S["added"], 16 * SQ * e)
                for q in range(SQ):
                    pool.wait_ge(S["ye"], SQ * e + q + 1)
                    pool.indirect_dma_start(
                        out, bass.IndirectOffsetOnAxis(ap=tok[e % 2][:, q:q + 1], axis=0),
                        ye[e % 2][:, q], None, bounds_check=TOKENS - 1, oob_is_err=False,
                        compute_op=ALU.add).then_inc(S["added"], 16)


def layout(x, i):
    import numpy as np
    d = {k: np.asarray(w) for k, w in i.items()}
    x = np.asarray(x)
    o = {}
    order = np.minimum(np.arange(NT * G), B - 1)
    fr = np.stack([x[:, n * HOP:n * HOP + FRAME] for n in range(T)], 1)[order]
    o["frames"] = fr.reshape(NT * R, FRAME).T
    mel = d["L0_tok_mel_filters"].T
    o["melT"] = np.concatenate([mel, mel], 0)
    o["dct"] = d["L0_tok_dct"]
    o["w_proj"] = d["L0_tok_w_proj"]
    o["b_proj"] = d["L0_tok_b_proj"][None]

    def chunks(w, extra=None):
        w = w.reshape(2, DC, -1).transpose(1, 0, 2)
        if extra is not None:
            w = np.concatenate([w, np.broadcast_to(extra, (1, 2, w.shape[2]))], 0)
        return w

    o["wlin"] = chunks(d["L0_attn_W_lin"].T, d["L0_attn_b_lin"])
    pad = lambda w: np.concatenate([w, np.zeros((5 * 128 - 3 * D,) + w.shape[1:], w.dtype)], 0)
    o["taps"] = pad(d["L0_attn_conv_w"][:, 0]).reshape(5, 128, KW).transpose(1, 0, 2)
    o["tapb"] = pad(d["L0_attn_conv_b"]).reshape(5, 128).T
    o["hfil"] = d["L0_attn_h_param"][:, :, :T].reshape(2, 2, DC, T).transpose(2, 0, 1, 3)
    o["alph"] = d["L0_attn_alphas"].reshape(2, DC).T
    o["winb"] = d["L0_attn_win_b"].reshape(2, DC).T
    o["bmat"] = d["L0_attn_Bmat"].reshape(1, 2, D)
    o["wout"] = chunks(d["L0_attn_W_out"].T, d["L0_attn_b_out"])
    o["ln1"] = d["L0_ffn_ln1_w"].reshape(2, DC).T
    o["ln2"] = d["L0_ffn_ln2_w"].reshape(2, DC).T
    o["wqkv"] = chunks(d["L0_ffn_c_attn_w"].T)
    w = d["L0_ffn_c_proj_w"].T
    o["wo"] = np.concatenate([w, np.zeros((64, D), w.dtype)], 0).reshape(2, 128, D).transpose(1, 0, 2)
    o["wgate"] = chunks(d["L0_ffn_w_g"].T)
    o["c_fc"] = d["L0_ffn_c_fc"]
    o["c_proj_e"] = d["L0_ffn_c_proj_e"]
    return o


SHAPES = {"fwd": (R, 3, FC), "coef": (T, 3, FC), "inv": (FC, 3, R), "sel": (R, G, HG * T)}


def kernel(x, **inputs):
    import numpy as np
    import concourse.bacc as bacc
    from concourse.bass_utils import run_bass_kernel_spmd

    nc = bacc.Bacc("TRN2", target_bir_lowering=False, num_devices=1)
    arrays, a = {}, {}
    for name, value in {**layout(x, inputs), **constants()}.items():
        value = np.ascontiguousarray(value).reshape(SHAPES.get(name, value.shape))
        arrays["in_" + name] = value
        a[name] = nc.dram_tensor("in_" + name, value.shape, mybir.dt.from_np(value.dtype), kind="ExternalInput").ap()
    out = nc.dram_tensor("out_0", (TOKENS, D), F32, kind="ExternalOutput").ap()
    tower(nc, a, out)
    r = run_bass_kernel_spmd(nc, [arrays], core_ids=[0])
    return r.results[0]["out_0"].reshape(B, T, D)
```

```python
from contextlib import ExitStack

import concourse.bass as bass
from concourse import mybir

ALU = mybir.AluOpType
ACT = mybir.ActivationFunctionType
AX = mybir.AxisListType
F32 = mybir.dt.float32
F32R = mybir.dt.float32r
BF16 = mybir.dt.bfloat16
U32 = mybir.dt.uint32

B, T, D = 64, 25, 192
G = 5
R = G * T
NT = -(-B // G)
LAST = (B - (NT - 1) * G) * T
TOKENS = B * T
FRAME, HOP, BINS, MELS, MFCC = 100, 160, 51, 40, 13
DC = D // 2
LANES = 7
KW = 3
ZC = [128, 128, 128, 128, 64]
NF = 2 * T - 1
FR = 3 * (NF // 2) + 1
FC = -(-G * FR // 3)
HEADS, HD = 12, 16
HG = 4
NG = HEADS // HG
GD = HG * HD
E, TOPK, FF = 8, 2, 4 * D
CAP = TOPK * TOKENS // E
SQ = 4
SR = CAP // SQ
MC = FF // 128
ROW = D + 4
NOWHERE = float(1 << 22)
EPS = 1e-5
SCALE = HD ** -0.5
MASKED = -1e30


def constants():
    import numpy as np
    c = {}
    n = np.arange(FRAME)
    window = 0.54 - 0.46 * np.cos(2.0 * np.pi * n / (FRAME - 1))
    ang = 2.0 * np.pi * np.outer(n, np.arange(BINS)) / FRAME
    c["dft"] = np.concatenate([np.cos(ang), -np.sin(ang)], 1) * window[:, None]
    t = np.arange(T)
    fwd, coef, inv = [np.ones(T)], [np.ones(T)], [np.ones(T) / NF]
    for f in range(1, NF // 2 + 1):
        co, si = np.cos(2 * np.pi * f * t / NF), np.sin(2 * np.pi * f * t / NF)
        fwd += [co - si, co, -si]
        coef += [co, -si - co, co - si]
        inv += [2 * (co - si) / NF, -2 * si / NF, -2 * co / NF]
    fwd, coef, inv = np.array(fwd), np.array(coef), np.array(inv)
    A = np.zeros((R, 3 * FC)); H = np.zeros((T, 3 * FC)); V = np.zeros((3 * FC, R))
    for b in range(G):
        r, k = slice(b * T, b * T + T), slice(b * FR, b * FR + FR)
        A[r, k] = fwd.T
        H[:, k] = coef.T
        V[k, r] = inv
    c["fwd"], c["coef"] = A, H
    c["inv"] = V.reshape(3, FC, R).transpose(1, 0, 2).reshape(FC, 3 * R)
    c["time"] = np.tile(np.linspace(0.0, 1.0, 512, dtype=np.float32)[:T], (DC, 1))
    c["ident"] = np.eye(128)
    head_of_row = (np.arange(128) % GD) // HD
    c["kmask"] = (head_of_row[:, None] == np.repeat(np.arange(HG), T)[None]) * 1.0
    sel = np.zeros((R, G, HG * T))
    for b in range(G):
        for h in range(HG):
            for k in range(T):
                sel[b * T + k, b, h * T + k] = 1.0
    c["sel"] = sel.reshape(R, -1)
    vh = (np.arange(D) % GD) // HD
    c["vmask"] = (np.repeat(np.arange(HG), T)[:, None] == vh[None]) * 1.0
    q = np.arange(R) % T
    c["causal"] = np.where(np.tile(np.arange(T), HG)[:, None] > q[None], MASKED, 0.0)
    c["before"] = (np.arange(R)[:, None] < np.arange(R)[None]) * 1.0
    c["expert"] = np.tile(np.arange(E), (128, 1))
    c["token"] = np.arange(R)[:, None] + R * np.arange(NT)[None]
    return {k: np.ascontiguousarray(v, dtype=np.float32) for k, v in c.items()}


PACKS = {
    "tok": [("dft", FRAME, 2 * BINS), ("melT", 2 * BINS, MELS), ("dct", MFCC, MELS), ("w_proj", MFCC, D),
            ("tokw", MELS + 1, D)],
    "lin": [("ident", 128, 128), ("wlin", DC + 1, 2, 3 * D), ("taps", 128, 5, KW), ("tapb", 128, 5)],
    "hyena": [("hfil", DC, 2, 2, T), ("alph", DC, 2), ("winb", DC, 2), ("bmat", 1, 2, D), ("time", DC, T),
              ("coef", T, 3, FC), ("fwd", R, 3, FC), ("inv", FC, 3, R), ("wout", DC + 1, 2, D)],
    "ffn": [("ln1", DC, 2), ("ln2", DC, 2), ("wqkv", DC, 2, 3 * D), ("wo", 128, 2, D), ("kmask", 128, HG * T),
            ("sel", R, G, HG * T), ("vmask", HG * T, D), ("causal", HG * T, R), ("before", R, R),
            ("expert", 128, E), ("token", R, NT), ("wgate", DC, 2, E)],
}


def size(dims):
    n = 1
    for d in dims:
        n *= d
    return n


def tower(nc, a, out):
    with ExitStack() as ctx:
        def sb(name, shape, dt=F32):
            return ctx.enter_context(nc.sbuf_tensor(name, shape, dt))

        S = {}

        def sem(name):
            S[name] = ctx.enter_context(nc.semaphore("s_" + name))
            return S[name]

        slots = nc.dram_tensor("slots", [E * CAP, ROW], F32).ap()

        frames = sb("frames", [FRAME, NT * R])
        pack, view = {}, {}
        for group, items in PACKS.items():
            pack[group] = sb("pack_" + group, [128, sum(size(dims) for _, _, *dims in items)])
            at_col = 0
            for name, rows, *dims in items:
                w = pack[group][0:rows, at_col:at_col + size(dims)]
                at_col += size(dims)
                if len(dims) == 2:
                    w = w.rearrange("p (a b) -> p a b", a=dims[0])
                elif len(dims) == 3:
                    w = w.rearrange("p (a b c) -> p a b c", a=dims[0], b=dims[1])
                view[name] = w
        dft, melT, dct, wtok, tokw = (view[n] for n in ("dft", "melT", "dct", "w_proj", "tokw"))
        ident, wlin, taps, tapb = (view[n] for n in ("ident", "wlin", "taps", "tapb"))
        hfil, alph, winb, bmat, times = (view[n] for n in ("hfil", "alph", "winb", "bmat", "time"))
        coef, fwd, inv, wout = (view[n] for n in ("coef", "fwd", "inv", "wout"))
        ln1, ln2, wqkv, wo, kmask, sel = (view[n] for n in ("ln1", "ln2", "wqkv", "wo", "kmask", "sel"))
        vmask, causal, before, expert = (view[n] for n in ("vmask", "causal", "before", "expert"))
        token, wgate = view["token"], view["wgate"]
        hdec = sb("hdec", [DC, 2, T])
        hT = sb("hT", [T, 2, D])
        habs = sb("habs", [T, 2])
        hrec = sb("hrec", [T, 2])
        hcoef = sb("hcoef", [FC, 2, 3, D])
        identb = sb("identb", [128, 128], BF16)
        causalb = sb("causalb", [HG * T, R], BF16)
        beforeb = sb("beforeb", [R, R], BF16)
        onesb = sb("onesb", [R, R], BF16)
        wfc = sb("wfc", [DC, 2, 2, FF])
        wpr = sb("wpr", [128, 2, MC, D])
        wfch = sb("wfch", [DC, 2, 2, FF], F32R)
        wfcl = sb("wfcl", [DC, 2, 2, FF], F32R)
        wprh = sb("wprh", [128, 2, MC, D], F32R)
        wprl = sb("wprl", [128, 2, MC, D], F32R)
        epsc = sb("epsc", [128, 2])
        fill = sb("fill", [SR, SQ, ROW])

        def two(name, shape, dt=F32):
            x = sb(name, [shape[0], 2] + shape[1:], dt)
            return [x[:, p] for p in range(2)]

        early = ExitStack()
        late = sb

        def sb(name, shape, dt=F32):
            return early.enter_context(nc.sbuf_tensor(name, shape, dt))


        sq = two("sq", [2 * BINS, R])
        logmel = two("logmel", [64, R])
        h0a = sb("h0", [R, 3, D])
        h0 = [h0a[:, n] for n in range(3)]
        u = two("u", [R, D])
        uT = two("uT", [DC + 1, 2, R])
        z = two("z", [128, 5, G, T + KW - 1])
        y = two("y", [128, 5, R])
        early.close()
        sb = late
        hidh = sb("hidh", [128, MC, CAP], F32R)
        hidl = sb("hidl", [128, MC, CAP], F32R)
        ex = two("ex", [R, 2, D])
        nmax = two("nmax", [R, 2])
        ssum = two("ssum", [R, 2])
        rsum = two("rsum", [R, 2])
        v = two("v", [R, D])
        prod = sb("prod", [FC, 3, D])
        gate = sb("gate", [R, D])
        vT = two("vT", [DC + 1, 2, R])
        hv = sb("hv", [R, D])
        h1 = two("h1", [R, D])
        xp = two("xp", [R, D])
        an = two("an", [R, D])
        stat = sb("stat", [R, 3, 6])
        mv = sb("mv", [R, 3, 2])
        lnv = sb("lnv", [R, 4])
        rstd = sb("rstd", [R, 4])
        var2 = sb("var2", [R, 1])
        aT = two("aT", [DC, 2, R])
        qT = sb("qT", [128, 2, R])
        sT = sb("sT", [HG * T, NG, R])
        kx = sb("kx", [128, 2, G, HG * T])
        vth = sb("vth", [R, D], F32R)
        vtl = sb("vtl", [R, D], F32R)
        vtr = sb("vtr", [R, D])
        selr = sb("selr", [R, G, HG * T], F32R)
        vx = sb("vx", [HG * T, G, D])
        smax = sb("smax", [R, HEADS])
        sc = sb("sc", [R, HEADS, T])
        es = sb("es", [R, HEADS, T])
        psm = sb("psm", [R, HEADS])
        prc = sb("prc", [R, HEADS])
        pn = sb("pn", [R, HEADS, T])
        pT = sb("pT", [HG * T, NG, R])
        yT = sb("yT", [128, 2, R])
        h2 = two("h2", [R, D])
        base = two("base", [R, D])
        xl = two("xl", [R, ROW])
        xlT = sb("xlT", [DC, 2, R])
        top = two("top", [R, 8])
        topi = two("topi", [R, 8], U32)
        ef = two("ef", [R, 2])
        diff = sb("diff", [R, 1])
        ed = sb("ed", [R, 1])
        den = sb("den", [R, 1])
        oh = sb("oh", [R, 2, E])
        chosen = two("chosen", [R, E], BF16)
        total = two("total", [R, E], BF16)
        junk = sb("junk", [R, 2, E])
        slot = sb("slot", [R, 2])
        over = sb("over", [R, 2])
        at = sb("at", [R, 2])
        row0 = sb("row0", [R, 2])
        atf = sb("atf", [R, 2])
        atu = two("atu", [R, 2], U32)
        xe = two("xe", [SR, SQ, ROW])
        xeTh = sb("xeTh", [DC, 2, CAP], F32R)
        xeTl = sb("xeTl", [DC, 2, CAP], F32R)
        gelu = two("gelu", [128, CAP])
        ye = two("ye", [SR, SQ, D])
        first = sb("first", [SR, SQ])
        wa = sb("wa", [SR, SQ])
        wb = sb("wb", [SR, SQ])
        wt = two("wt", [SR, SQ])
        tok = two("tok", [SR, SQ], U32)

        PB = [ctx.enter_context(nc.psum_tensor(f"bank{i}", [128, 512], F32)) for i in range(8)]
        pspec, pmel, ptok = PB[0][0:2 * BINS, 0:R], PB[0][0:MELS, 0:R], PB[0][0:R, 0:D]
        puT = PB[0][0:DC, 0:2 * R].rearrange("p (c n) -> p c n", c=2)
        pz = PB[1][:, 0:4 * R].rearrange("p (c n) -> p c n", c=4)
        px = PB[1][0:R, 0:2 * D]
        pz4 = PB[2][0:64, 0:R]
        pv = PB[2][0:R, 0:D]
        pf01, pf2, py = PB[3][0:FC, 0:2 * D], PB[4][0:FC, 0:D], PB[4][0:R, 0:D]
        pvT = PB[3][0:DC, 0:2 * R].rearrange("p (c n) -> p c n", c=2)
        po = PB[4][0:R, 0:D]
        paT = PB[5][0:DC, 0:2 * R].rearrange("p (c n) -> p c n", c=2)
        pq = PB[5][:, 0:2 * R].rearrange("p (c n) -> p c n", c=2)
        pvv = PB[5][0:R, 256:256 + D]
        pk = PB[6][:, 0:2 * R].rearrange("p (c n) -> p c n", c=2)
        psT = [PB[n][0:HG * T, x * R:(x + 1) * R] for n, x in ((5, 0), (6, 0), (5, 1))]
        ps = PB[6][0:R, 0:NG * HG * T]
        ppT = PB[5][0:HG * T, 0:NG * R].rearrange("p (g n) -> p g n", g=NG)
        pvx = PB[7][0:HG * T, 0:2 * D].rearrange("p (b d) -> p b d", b=2)
        pyT = PB[7][:, 0:2 * R].rearrange("p (c n) -> p c n", c=2)
        pao = PB[7][0:R, 0:D]
        pxT = PB[2][0:DC, 0:2 * R].rearrange("p (c n) -> p c n", c=2)
        pg, ppos = PB[2][0:R, 0:E], PB[2][0:R, 0:E]

        for name in ("in_tok", "in_frames", "in_lin", "in_hyena", "in_ffn", "in_exp0", "in_exp1", "filled", "stored0", "stored1", "scattered0", "scattered1",
                     "in_slots0", "in_slots1", "added", "zeroed", "bf",
                     "dctw", "tokw", "dec", "decb", "fil", "filT", "habs", "hrec", "hT", "hc0", "hc1", "hcoef0", "hcoef1", "hb",
                     "spec", "sq", "mel", "logmel", "tok", "h0", "st0", "var0", "lnv0", "r0", "u", "uT", "uTs",
                     "z", "zs", "c1", "c2", "conv", "xT", "vT0", "nmax", "ex", "rsum", "v0",
                     "f0", "f1", "prod0", "prod1", "y0", "y1", "g0", "g1", "v1", "v2",
                     "vT", "vTs", "o", "hv", "h1", "st1", "var1", "lnv1", "r1", "xp", "var2", "lnv2", "r2", "an",
                     "aT", "aTs", "k", "qv", "qs", "vtr", "vtl", "kx", "vx0", "vx1", "vx2", "vxs0", "vxs1", "vxs2",
                     "sT", "sTs", "s", "smax", "sc", "es", "psm", "prc", "pn", "pT", "pTs", "yT", "yTs", "ao", "h2", "base",
                     "st2", "var3", "lnv3", "r3", "xl", "xlT", "xlTs", "g", "top", "topi", "diff", "ed", "den",
                     "w0", "meta", "ef", "oh", "chosen", "total", "pos", "slot", "row0", "over", "at", "atf", "atu",
                     "wfch", "wfcl", "wprh", "wprl", "xeT", "xeTh", "xeTl", "fc", "gelu", "hidl", "pr", "ye", "wfirst", "wab", "wt", "tki"):
            sem(name)

        def need(eng, name, value):
            if value > 0:
                eng.wait_ge(S[name], value)

        def lanes(j):
            return [j - n for n in range(LANES)]

        def ok(i):
            return 0 <= i < NT

        def yv(i, c):
            return y[i % 2][0:ZC[c], c].rearrange("p (b t) -> p b t", t=T)

        def zv(i, c, k):
            return z[i % 2][0:ZC[c], c, :, k:k + T]

        block = ctx.enter_context(nc.Block())

        @block.sync
        def _(sp):
            def load(dst, src, name):
                sp.dma_start(dst, src).then_inc(S[name], 16)

            load(pack["tok"][:], a["tok"], "in_tok")
            load(frames[:, 0:R], a["frames"][:, 0:R], "in_tok")
            load(pack["lin"][:], a["lin"], "in_lin")
            load(pack["hyena"][:], a["hyena"], "in_hyena")
            load(frames[:, R:], a["frames"][:, R:], "in_frames")
            load(pack["ffn"][:], a["ffn"], "in_ffn")
            need(sp, "zeroed", 3)
            for e in range(E):
                sp.dma_start(slots[e * CAP:(e + 1) * CAP, :].rearrange("(q p) c -> p q c", p=SR), fill[:])\
                    .then_inc(S["filled"], 16)

            def weights(e):
                if e >= 2:
                    sp.wait_ge(S["wfcl"], e - 1)
                    sp.wait_ge(S["wprl"], e - 1)
                load(wfc[:, e % 2], a["c_fc"][e].rearrange("(k p) f -> p k f", p=DC), f"in_exp{e % 2}")
                load(wpr[:, e % 2], a["c_proj_e"][e].rearrange("(m p) d -> p m d", p=128), f"in_exp{e % 2}")

            weights(0)
            weights(1)
            for i in range(NT):
                rows = R if i < NT - 1 else LAST
                need(sp, "base", i + 1)
                sp.dma_start(out[i * R:i * R + rows, :], base[i % 2][0:rows, :]).then_inc(S[f"stored{i % 2}"], 16)
            for p in range(2):
                sp.wait_ge(S[f"scattered{p}"], 16 * TOPK * ((NT + 1 - p) // 2))
            for e in range(E):
                if e >= 2:
                    sp.wait_ge(S["wt"], e - 1)
                    sp.wait_ge(S["xeT"], e - 1)
                    sp.wait_ge(S["tki"], e - 1)
                sp.dma_start(xe[e % 2], slots[e * CAP:(e + 1) * CAP, :].rearrange("(q p) c -> p q c", p=SR))\
                    .then_inc(S[f"in_slots{e % 2}"], 16)
                if 1 <= e < E - 1:
                    weights(e + 1)
            sp.wait_ge(S["added"], 16 * SQ * E)

        @block.tensor
        def _(pe):
            mm, tr = pe.matmul, pe.transpose

            pe.wait_ge(S["in_tok"], 16 * 2)
            mm(PB[0][0:MELS, 0:D], dct[:], wtok[:], start=True, stop=True).then_inc(S["dctw"], 1)
            pe.wait_ge(S["zeroed"], 3)
            pe.wait_ge(S["tokw"], 1)

            def a_spec(i):
                if i == 1:
                    pe.wait_ge(S["in_frames"], 16)
                need(pe, "uTs", i)
                mm(pspec, dft[:], frames[:, i * R:(i + 1) * R], start=True, stop=True).then_inc(S["spec"], 1)

            def a_mel(i):
                pe.wait_ge(S["sq"], i + 1)
                mm(pmel, melT[:], sq[i % 2], start=True, stop=True).then_inc(S["mel"], 1)

            def a_tok(i):
                pe.wait_ge(S["logmel"], i + 1)
                mm(ptok, logmel[i % 2][0:MELS + 1, :], tokw[:], start=True, stop=True).then_inc(S["tok"], 1)

            def a_uT(i):
                if i == 0:
                    pe.wait_ge(S["in_lin"], 16)
                pe.wait_ge(S["u"], i + 1)
                for k in range(2):
                    last = tr(puT[:, k], u[i % 2][:, k * DC:(k + 1) * DC], ident[0:R, 0:R])
                last.then_inc(S["uT"], 1)

            def a_z(i):
                need(pe, "ex", i)
                need(pe, "v0", i)
                need(pe, "topi", i - 3)
                pe.wait_ge(S["uTs"], i + 1)
                for c, m in enumerate(ZC):
                    dst = pz[:, c] if c < 4 else pz4
                    for k in range(2):
                        kk = DC + k
                        last = mm(dst, wlin[0:kk, k, c * 128:c * 128 + m], uT[i % 2][0:kk, k],
                                  start=k == 0, stop=k == 1)
                last.then_inc(S["z"], 1)

            def a_xT(i):
                pe.wait_ge(S["conv"], i + 1)
                for c in range(3):
                    last = tr(px[:, c * 128:(c + 1) * 128], y[i % 2][:, c], ident[:])
                last.then_inc(S["xT"], 1)
                need(pe, "slot", i - 3)
                tr(pv[:, 0:128], y[i % 2][:, 3], ident[:])
                tr(pv[:, 128:192], y[i % 2][0:64, 4], ident[0:64, 0:64]).then_inc(S["vT0"], 1)

            def b_f(i, o):
                if i == 0 and o == 0:
                    pe.wait_ge(S["in_hyena"], 16)
                if i == 0 and o == 0:
                    pe.wait_ge(S["hcoef1"], 1)
                if o == 0:
                    need(pe, "vTs", i)
                    need(pe, "h1", i)
                pe.wait_ge(S[f"v{o}"], i + 1)
                for c in range(3):
                    last = mm(pf01[:, c * D:(c + 1) * D] if c < 2 else pf2, fwd[:, c], v[i % 2],
                              start=True, stop=True)
                last.then_inc(S[f"f{o}"], 1)

            def b_y(i, o):
                pe.wait_ge(S[f"prod{o}"], i + 1)
                for c in range(3):
                    last = mm(py, inv[:, c], prod[:, c], start=c == 0, stop=c == 2)
                last.then_inc(S[f"y{o}"], 1)

            def b_vT(i):
                pe.wait_ge(S["v2"], i + 1)
                for k in range(2):
                    last = tr(pvT[:, k], v[i % 2][:, k * DC:(k + 1) * DC], ident[0:R, 0:R])
                last.then_inc(S["vT"], 1)

            def b_o(i):
                pe.wait_ge(S["vTs"], i + 1)
                for k in range(2):
                    last = mm(po, vT[i % 2][0:DC + k, k], wout[0:DC + k, k], start=k == 0, stop=k == 1)
                last.then_inc(S["o"], 1)

            def c_aT(i):
                if i == 0:
                    pe.wait_ge(S["in_ffn"], 16)
                need(pe, "pTs", i)
                pe.wait_ge(S["an"], i + 1)
                for k in range(2):
                    last = tr(paT[:, k], an[i % 2][:, k * DC:(k + 1) * DC], ident[0:R, 0:R])
                last.then_inc(S["aT"], 1)

            def c_qkv(i):
                pe.wait_ge(S["aTs"], i + 1)
                need(pe, "sc", i)
                for n, dst in ((1, pk), (0, pq)):
                    for c, m in ((0, 128), (1, 64)):
                        for k in range(2):
                            last = mm(dst[0:m, c], wqkv[:, k, n * D + c * 128:n * D + c * 128 + m], aT[i % 2][:, k],
                                      start=k == 0, stop=k == 1)
                    if n:
                        last.then_inc(S["k"], 1)
                for k in range(2):
                    last = mm(pvv, aT[i % 2][:, k], wqkv[:, k, 2 * D:], start=k == 0, stop=k == 1)
                last.then_inc(S["qv"], 1)

            def c_vx(i, n):
                if i == 0 and n == 0:
                    pe.wait_ge(S["bf"], 1)
                if n == 0:
                    need(pe, "h2", i)
                    pe.wait_ge(S["vtl"], i + 1)
                else:
                    pe.wait_ge(S[f"vxs{n - 1}"], i + 1)
                for b in range(2 * n, min(2 * n + 2, G)):
                    mm(pvx[:, b - 2 * n], selr[:, b], vth[:], start=True, stop=False)
                    last = mm(pvx[:, b - 2 * n], selr[:, b], vtl[:], start=False, stop=True)
                last.then_inc(S[f"vx{n}"], 1)

            def c_sT(i):
                if i == 0:
                    pe.wait_ge(S["bf"], 1)
                pe.wait_ge(S["qs"], i + 1)
                pe.wait_ge(S["vtr"], i + 1)
                pe.wait_ge(S["kx"], i + 1)
                for g in range(NG):
                    r0, c = GD * (g % 2), g // 2
                    mm(psT[g], identb[0:HG * T, 0:HG * T], causalb[:], start=True, stop=False)
                    for b in range(G):
                        last = mm(psT[g][:, b * T:(b + 1) * T], kx[r0:r0 + GD, c, b], qT[r0:r0 + GD, c, b * T:(b + 1) * T],
                                  start=False, stop=b == G - 1)
                last.then_inc(S["sT"], 1)

            def c_s(i):
                pe.wait_ge(S["sTs"], i + 1)
                for g in range(NG):
                    last = tr(ps[:, g * HG * T:(g + 1) * HG * T], sT[:, g], ident[0:HG * T, 0:HG * T])
                last.then_inc(S["s"], 1)

            def c_pT(i):
                pe.wait_ge(S["pn"], i + 1)
                for g in range(NG):
                    last = tr(ppT[:, g], pn[:, g * HG:(g + 1) * HG], ident[0:R, 0:R])
                last.then_inc(S["pT"], 1)

            def c_yT(i):
                pe.wait_ge(S["pTs"], i + 1)
                pe.wait_ge(S["vxs2"], i + 1)
                for g in range(NG):
                    r0 = GD * (g % 2)
                    for b in range(G):
                        last = mm(pyT[r0:r0 + GD, g // 2, b * T:(b + 1) * T], vx[:, b, g * GD:(g + 1) * GD],
                                  pT[:, g, b * T:(b + 1) * T], start=True, stop=True)
                last.then_inc(S["yT"], 1)

            def c_ao(i):
                pe.wait_ge(S["yTs"], i + 1)
                mm(pao, yT[:, 0], wo[:, 0], start=True, stop=False)
                mm(pao, yT[0:64, 1], wo[0:64, 1], start=False, stop=True).then_inc(S["ao"], 1)

            def c_xlT(i):
                need(pe, "v0", min(i + 4, NT))
                pe.wait_ge(S["xl"], i + 1)
                for k in range(2):
                    last = tr(pxT[:, k], xl[i % 2][:, k * DC:(k + 1) * DC], ident[0:R, 0:R])
                last.then_inc(S["xlT"], 1)

            def c_gate(i):
                pe.wait_ge(S["xlTs"], i + 1)
                for k in range(2):
                    last = mm(pg, xlT[:, k], wgate[:, k], start=k == 0, stop=k == 1)
                last.then_inc(S["g"], 1)

            def c_pos(i):
                need(pe, "zs", min(i + 5, NT))
                pe.wait_ge(S["topi"], i + 1)
                pe.wait_ge(S["chosen"], i + 1)
                need(pe, "total", i)
                last = mm(ppos, beforeb[:], chosen[i % 2], start=True, stop=i == 0)
                if i:
                    last = mm(ppos, onesb[:], total[(i - 1) % 2], start=False, stop=True)
                last.then_inc(S["pos"], 1)

            def h_filT(i):
                pe.wait_ge(S["in_lin"], 16)
                pe.wait_ge(S["fil"], 1)
                for o in range(2):
                    for k in range(2):
                        last = tr(PB[7][0:T, o * D + k * DC:o * D + (k + 1) * DC], hfil[:, o, k], ident[0:DC, 0:DC])
                last.then_inc(S["filT"], 1)

            def h_hc(i, o):
                pe.wait_ge(S["hb"], 1)
                if o:
                    pe.wait_ge(S["hcoef0"], 1)
                for c in range(3):
                    last = mm((pf01[:, c * D:(c + 1) * D] if c < 2 else pf2), coef[:, c], hT[:, o],
                              start=True, stop=True)
                last.then_inc(S[f"hc{o}"], 1)

            for j in range(NT + LANES - 1):
                t, i, b, c, k, d, w = lanes(j)
                if ok(d): c_vx(d, 2)
                if ok(b): a_z(b)
                if ok(d): c_pT(d)
                if ok(c): b_y(c, 0)
                if ok(d): c_yT(d)
                if ok(k): c_aT(k)
                if ok(c): b_f(c, 1)
                if b == 0: h_hc(b, 0)
                if ok(w): c_pos(w)
                if ok(i): a_mel(i)
                if ok(k): c_qkv(k)
                if ok(i): a_tok(i)
                if i == 0: h_filT(i)
                if ok(d): c_ao(d)
                if ok(c): b_y(c, 1)
                if b == 0: h_hc(b, 1)
                if ok(k): c_sT(k)
                if ok(b): a_xT(b)
                if ok(k): c_vx(k, 0)
                if ok(c): b_vT(c)
                if ok(k): c_s(k)
                if ok(d): c_xlT(d)
                if ok(i): a_uT(i)
                if ok(c): b_o(c)
                if ok(k): c_vx(k, 1)
                if ok(d): c_gate(d)
                if ok(t): a_spec(t)
                if ok(b): b_f(b, 0)

            def e_xT(e):
                need(pe, "xeTl", e)
                pe.wait_ge(S[f"in_slots{e % 2}"], 16 * (e // 2 + 1))
                for k in range(2):
                    for q in range(SQ):
                        last = tr(PB[k][0:DC, q * SR:(q + 1) * SR], xe[e % 2][:, q, k * DC:(k + 1) * DC],
                                  ident[0:SR, 0:SR])
                last.then_inc(S["xeT"], 1)

            def e_fc(e):
                pe.wait_ge(S["xeTl"], e + 1)
                pe.wait_ge(S["wfcl"], e + 1)
                for m in range(MC):
                    n = e * MC + m
                    need(pe, "gelu", n - 3)
                    ms = slice(m * 128, (m + 1) * 128)
                    for k in range(2):
                        dst = PB[2 + n % 4][:, 0:CAP]
                        mm(dst, wfch[:, e % 2, k, ms], xeTh[:, k], start=k == 0, stop=False)
                        mm(dst, wfch[:, e % 2, k, ms], xeTl[:, k], start=False, stop=False)
                        last = mm(dst, wfcl[:, e % 2, k, ms], xeTh[:, k], start=False, stop=k == 1)
                    last.then_inc(S["fc"], 1)

            def e_pr(e):
                pe.wait_ge(S["wprl"], e + 1)
                for q in range(SQ):
                    if q % 2 == 0:
                        need(pe, "ye", SQ * (e - 1) + q + 2)
                    dst = PB[6 + q // 2][0:SR, (q % 2) * D:(q % 2 + 1) * D]
                    qs = slice(q * SR, (q + 1) * SR)
                    for m in range(MC):
                        if q == 0:
                            pe.wait_ge(S["hidl"], e * MC + m + 1)
                        mm(dst, hidh[:, m, qs], wprh[:, e % 2, m], start=m == 0, stop=False)
                        mm(dst, hidh[:, m, qs], wprl[:, e % 2, m], start=False, stop=False)
                        last = mm(dst, hidl[:, m, qs], wprh[:, e % 2, m], start=False, stop=m == MC - 1)
                    last.then_inc(S["pr"], 1)

            pe.wait_ge(S["slot"], NT)
            e_xT(0)
            for e in range(E):
                e_fc(e)
                if e + 1 < E:
                    e_xT(e + 1)
                e_pr(e)

        @block.scalar
        def _(act):
            f = act.activation

            def rstd_of(name, n, src, i):
                act.wait_ge(S[{0: "var0", 1: "var1", 2: "var2", 3: "var3"}[n]], i + 1)
                f(lnv[:, n:n + 1], src, ACT.Ln, bias=epsc[0:R, 0:1]).then_inc(S[f"lnv{n}"], 1)
                act.wait_ge(S[f"lnv{n}"], i + 1)
                f(rstd[:, n:n + 1], lnv[:, n:n + 1], ACT.Exp, scale=-0.5).then_inc(S[f"r{n}"], 1)

            act.preload_act_table_set("natural_log_exp_and_others")
            act.wait_ge(S["zeroed"], 3)
            act.wait_ge(S["dctw"], 1)
            f(tokw[0:MELS, :], PB[0][0:MELS, 0:D], ACT.Copy).then_inc(S["tokw"], 1)

            def a_sq(i):
                act.wait_ge(S["spec"], i + 1)
                need(act, "mel", i - 1)
                f(sq[i % 2], pspec, ACT.Square).then_inc(S["sq"], 1)

            def a_log(i):
                act.wait_ge(S["mel"], i + 1)
                need(act, "tok", i - 1)
                f(logmel[i % 2][0:MELS, :], pmel, ACT.Ln, bias=epsc[0:MELS, 1:2]).then_inc(S["logmel"], 1)

            def a_h0(i):
                act.wait_ge(S["tok"], i + 1)
                need(act, "hv", i - 2)
                f(h0[i % 3], ptok, ACT.Copy).then_inc(S["h0"], 1)

            def a_r(i):
                rstd_of("0", 0, mv[:, 0, 1:2], i)

            def a_uTs(i):
                act.wait_ge(S["uT"], i + 1)
                need(act, "z", i - 1)
                f(uT[i % 2][0:DC], puT, ACT.Copy).then_inc(S["uTs"], 1)

            def a_zs(i):
                act.wait_ge(S["z"], i + 1)
                need(act, "conv", i - 1)
                f(z[i % 2][:, 0:4].rearrange("p c b t -> p (c b) t")[:, :, KW - 1:],
                  pz.rearrange("p c (b t) -> p (c b) t", t=T), ACT.Copy)
                f(z[i % 2][0:64, 4, :, KW - 1:], pz4.rearrange("p (b t) -> p b t", t=T), ACT.Copy)\
                    .then_inc(S["zs"], 1)

            def a_conv1(i):
                act.wait_ge(S["zs"], i + 1)
                need(act, "vT0", i - 1)
                for c in range(5):
                    last = f(yv(i, c), zv(i, c, 0), ACT.Identity, scale=taps[0:ZC[c], c, 0:1], bias=tapb[0:ZC[c], c:c + 1])
                last.then_inc(S["c1"], 1)

            def b_an(i):
                act.wait_ge(S["xp"], i + 1)
                act.wait_ge(S["r2"], i + 1)
                need(act, "aT", i - 1)
                f(an[i % 2], xp[i % 2], ACT.Copy, scale=rstd[:, 2:3]).then_inc(S["an"], 1)

            def a_ex(i):
                act.wait_ge(S["nmax"], i + 1)
                need(act, "g1", i - 1)
                need(act, "rsum", i - 1)
                for o in range(2):
                    last = f(ex[i % 2][:, o], px[:, o * D:(o + 1) * D], ACT.Exp, bias=nmax[i % 2][:, o:o + 1],
                             accum_out=ssum[i % 2][:, o:o + 1])
                last.then_inc(S["ex"], 1)

            def b_vTs(i):
                act.wait_ge(S["vT"], i + 1)
                need(act, "o", i - 1)
                f(vT[i % 2][0:DC], pvT, ACT.Copy).then_inc(S["vTs"], 1)

            def b_r(i):
                rstd_of("1", 1, mv[:, 1, 1:2], i)

            def b_r2(i):
                rstd_of("2", 2, var2[:], i)

            def c_aTs(i):
                if i == 0:
                    act.wait_ge(S["in_ffn"], 16)
                act.wait_ge(S["aT"], i + 1)
                need(act, "qv", i - 1)
                for k in range(2):
                    last = f(aT[i % 2][:, k], paT[:, k], ACT.Copy, scale=ln1[:, k:k + 1])
                last.then_inc(S["aTs"], 1)

            def c_qs(i):
                act.wait_ge(S["qv"], i + 1)
                need(act, "sT", i)
                for c, m in ((0, 128), (1, 64)):
                    last = f(qT[0:m, c], pq[0:m, c], ACT.Copy)
                last.then_inc(S["qs"], 1)

            def c_sTs(i):
                act.wait_ge(S["sT"], i + 1)
                need(act, "s", i)
                f(sT[:, 0:NG:2], PB[5][0:HG * T, 0:2 * R].rearrange("p (g n) -> p g n", g=2), ACT.Copy)
                f(sT[:, 1], psT[1], ACT.Copy).then_inc(S["sTs"], 1)

            def c_vs(i):
                act.wait_ge(S["qv"], i + 1)
                need(act, "vx2", i)
                f(vth[:], pvv, ACT.Copy)
                f(vtr[:], pvv, ACT.Copy).then_inc(S["vtr"], 1)

            def c_es(i):
                act.wait_ge(S["sc"], i + 1)
                need(act, "pn", i)
                f(es[:], sc[:], ACT.Exp, scale=SCALE).then_inc(S["es"], 1)

            def c_pTs(i):
                act.wait_ge(S["pT"], i + 1)
                need(act, "yT", i)
                f(pT[:], ppT, ACT.Copy).then_inc(S["pTs"], 1)

            def c_yTs(i):
                act.wait_ge(S["yT"], i + 1)
                need(act, "ao", i)
                f(yT[:, 0], pyT[:, 0], ACT.Copy)
                f(yT[0:64, 1], pyT[0:64, 1], ACT.Copy).then_inc(S["yTs"], 1)

            def c_r(i):
                rstd_of("3", 3, mv[:, 2, 1:2], i)

            def c_xlTs(i):
                act.wait_ge(S["xlT"], i + 1)
                need(act, "g", i)
                for k in range(2):
                    last = f(xlT[:, k], pxT[:, k], ACT.Copy, scale=ln2[:, k:k + 1])
                last.then_inc(S["xlTs"], 1)

            def c_ed(i):
                act.wait_ge(S["diff"], i + 1)
                need(act, "w0", i)
                f(ed[:], diff[:], ACT.Exp).then_inc(S["ed"], 1)

            def h_dec(i):
                act.wait_ge(S["in_hyena"], 16)
                for k in range(2):
                    last = f(hdec[:, k], times[:], ACT.Exp, scale=alph[:, k:k + 1])
                last.then_inc(S["dec"], 1)

            def e_wh(e):
                act.wait_ge(S[f"in_exp{e % 2}"], 16 * 2 * (e // 2 + 1))
                need(act, "fc", MC * (e - 1))
                f(wfch[:, e % 2], wfc[:, e % 2], ACT.Copy).then_inc(S["wfch"], 1)
                need(act, "pr", SQ * (e - 1))
                f(wprh[:, e % 2], wpr[:, e % 2], ACT.Copy).then_inc(S["wprh"], 1)

            for j in range(NT + LANES - 1):
                t, i, b, c, k, d, w = lanes(j)
                if ok(b): a_zs(b)
                if ok(k): b_an(k)
                if ok(k): c_aTs(k)
                if ok(d): c_yTs(d)
                if ok(b): a_conv1(b)
                if ok(i): a_log(i)
                if ok(k): c_vs(k)
                if ok(i): a_h0(i)
                if ok(k): c_qs(k)
                if ok(d): c_r(d)
                if ok(i): a_r(i)
                if ok(k): c_sTs(k)
                if ok(c): b_vTs(c)
                if ok(d): c_xlTs(d)
                if t == 0: h_dec(t)
                if ok(i): a_uTs(i)
                if ok(k): c_es(k)
                if ok(b): a_ex(b)
                if ok(c): b_r(c)
                if ok(t): a_sq(t)
                if ok(k): c_pTs(k)
                if ok(c): b_r2(c)
                if ok(d): c_ed(d)

            def e_xTh(e):
                act.wait_ge(S["xeT"], e + 1)
                need(act, "fc", MC * e)
                for k in range(2):
                    f(xeTh[:, k], PB[k][0:DC, 0:CAP], ACT.Copy, scale=ln2[:, k:k + 1]).then_inc(S["xeTh"], 1)

            e_wh(0)
            e_xTh(0)
            for e in range(E):
                if e < E - 1: e_wh(e + 1)
                for m in range(MC):
                    n = e * MC + m
                    act.wait_ge(S["fc"], n + 1)
                    if m == 0:
                        need(act, "pr", SQ * e)
                    f(hidh[:, m], PB[2 + n % 4][:, 0:CAP], ACT.Gelu)
                    need(act, "hidl", n - 1)
                    f(gelu[n % 2], PB[2 + n % 4][:, 0:CAP], ACT.Gelu).then_inc(S["gelu"], 1)
                if e + 1 < E: e_xTh(e + 1)

        @block.vector
        def _(ve):
            tt, ts, stt = ve.tensor_tensor, ve.tensor_scalar, ve.scalar_tensor_tensor

            def layer_stats(n, src, i, var):
                ve.bn_stats(stat[:, n], src).then_inc(S[f"st{n}"], 1)
                ve.wait_ge(S[f"st{n}"], i + 1)
                ve.bn_aggr(mv[:, n], stat[:, n]).then_inc(S[var], 1)

            def a_stats(i):
                ve.wait_ge(S["h0"], i + 1)
                layer_stats(0, h0[i % 3], i, "var0")

            def a_u(i):
                ve.wait_ge(S["r0"], i + 1)
                need(ve, "uT", i - 1)
                need(ve, "v0", i - 1)
                ts(u[i % 2], h0[i % 3], mv[:, 0, 0:1], rstd[:, 0:1], ALU.subtract, ALU.mult).then_inc(S["u"], 1)

            def tap(i, k):
                for c in range(5):
                    last = stt(yv(i, c), zv(i, c, k), taps[0:ZC[c], c, k:k + 1], yv(i, c), ALU.mult, ALU.add)
                return last

            def a_conv2(i):
                ve.wait_ge(S["c1"], i + 1)
                tap(i, 1).then_inc(S["c2"], 1)

            def a_conv3(i):
                ve.wait_ge(S["c2"], i + 1)
                tap(i, 2).then_inc(S["conv"], 1)

            def a_nmax(i):
                ve.wait_ge(S["xT"], i + 1)
                ve.tensor_reduce(nmax[i % 2], px.rearrange("p (o d) -> p o d", o=2), AX.X, ALU.max, negate=True)\
                    .then_inc(S["nmax"], 1)

            def a_v0(i):
                ve.wait_ge(S["vT0"], i + 1)
                need(ve, "vT", i - 1)
                need(ve, "hv", i - 1)
                tt(v[i % 2], pv, u[i % 2], ALU.add).then_inc(S["v0"], 1)

            def a_rsum(i):
                ve.wait_ge(S["ex"], i + 1)
                ve.reciprocal(rsum[i % 2], ssum[i % 2]).then_inc(S["rsum"], 1)

            def b_prod(i, o):
                ve.wait_ge(S[f"f{o}"], i + 1)
                if o == 1:
                    ve.wait_ge(S["y0"], i + 1)
                else:
                    need(ve, "y1", i)
                tt(prod[:, 0:2].rearrange("p c d -> p (c d)"), pf01,
                   hcoef[:, o, 0:2].rearrange("p c d -> p (c d)"), ALU.mult)
                tt(prod[:, 2], pf2, hcoef[:, o, 2], ALU.mult).then_inc(S[f"prod{o}"], 1)

            def b_v(i, o):
                ve.wait_ge(S[f"y{o}"], i + 1)
                ve.wait_ge(S["rsum"], i + 1)
                stt(gate[:], ex[i % 2][:, o], rsum[i % 2][:, o:o + 1], py, ALU.mult, ALU.mult)\
                    .then_inc(S[f"g{o}"], 1)
                ve.wait_ge(S[f"g{o}"], i + 1)
                tt(v[i % 2], v[i % 2], gate[:], ALU.add).then_inc(S[f"v{o + 1}"], 1)

            def b_h1(i):
                ve.wait_ge(S["o"], i + 1)
                ve.wait_ge(S["hv"], i + 1)
                need(ve, "base", i - 1)
                tt(h1[i % 2], po, hv[:], ALU.add).then_inc(S["h1"], 1)
                ve.wait_ge(S["h1"], i + 1)
                layer_stats(1, h1[i % 2], i, "var1")

            def b_xp(i):
                ve.wait_ge(S["r1"], i + 1)
                stt(var2[:], mv[:, 1, 1:2], rstd[:, 1:2], rstd[:, 1:2], ALU.mult, ALU.mult).then_inc(S["var2"], 1)
                ts(xp[i % 2], h1[i % 2], mv[:, 1, 0:1], rstd[:, 1:2], ALU.subtract, ALU.mult).then_inc(S["xp"], 1)

            def c_kx(i):
                if i == 0:
                    ve.wait_ge(S["in_ffn"], 16)
                ve.wait_ge(S["k"], i + 1)
                need(ve, "sT", i)
                for c, m in ((0, 128), (1, 64)):
                    src = pk[0:m, c].rearrange("p (b k) -> p b k", k=T)[:, :, None, :].broadcast_to([m, G, HG, T])
                    msk = kmask[0:m].rearrange("p (h k) -> p h k", k=T)[:, None].broadcast_to([m, G, HG, T])
                    last = tt(kx[0:m, c].rearrange("p b (h k) -> p b h k", k=T), src, msk, ALU.mult)
                last.then_inc(S["kx"], 1)

            def c_vxs(i, n):
                if n == 0:
                    need(ve, "yT", i)
                ve.wait_ge(S[f"vx{n}"], i + 1)
                k = min(2, G - 2 * n)
                tt(vx[:, 2 * n:2 * n + k], pvx[:, 0:k], vmask[:, None, :].broadcast_to([HG * T, k, D]), ALU.mult)\
                    .then_inc(S[f"vxs{n}"], 1)

            def c_sc(i):
                ve.wait_ge(S["s"], i + 1)
                src = ps.rearrange("p (h k) -> p h k", k=T)
                ve.tensor_reduce(smax[:], src, AX.X, ALU.max).then_inc(S["smax"], 1)
                ve.wait_ge(S["smax"], i + 1)
                need(ve, "es", i)
                tt(sc[:], src, smax[:, :, None].broadcast_to([R, HEADS, T]), ALU.subtract).then_inc(S["sc"], 1)

            def c_pn(i):
                ve.wait_ge(S["es"], i + 1)
                need(ve, "pn", i)
                ve.tensor_reduce(psm[:], es[:], AX.X, ALU.add).then_inc(S["psm"], 1)
                ve.wait_ge(S["psm"], i + 1)
                ve.reciprocal(prc[:], psm[:]).then_inc(S["prc"], 1)

            def c_h2(i):
                ve.wait_ge(S["ao"], i + 1)
                need(ve, "base", i - 1)
                tt(h2[i % 2], pao, xp[i % 2], ALU.add).then_inc(S["h2"], 1)
                ve.wait_ge(S["h2"], i + 1)
                layer_stats(2, h2[i % 2], i, "var3")

            def c_xl(i):
                ve.wait_ge(S["r3"], i + 1)
                if i >= 2:
                    ve.wait_ge(S[f"scattered{i % 2}"], 16 * TOPK * (i // 2))
                need(ve, "xlT", i - 1)
                ts(xl[i % 2][:, 0:D], h2[i % 2], mv[:, 2, 0:1], rstd[:, 3:4], ALU.subtract, ALU.mult)\
                    .then_inc(S["xl"], 1)

            def c_route(i):
                p = i % 2
                ve.wait_ge(S["g"], i + 1)
                ve.max(top[p], pg).then_inc(S["top"], 1)
                ve.wait_ge(S["top"], i + 1)
                ve.max_index(topi[p], top[p], pg).then_inc(S["topi"], 1)
                tt(diff[:], top[p][:, 1:2], top[p][:, 0:1], ALU.subtract).then_inc(S["diff"], 1)
                ve.wait_ge(S["topi"], i + 1)
                ve.tensor_copy(ef[p], topi[p][:, 0:2]).then_inc(S["ef"], 1)
                ve.wait_ge(S["ef"], i + 1)
                for k in range(2):
                    last = ts(oh[:, k], expert[0:R], ef[p][:, k:k + 1], None, ALU.is_equal)
                last.then_inc(S["oh"], 1)
                ve.wait_ge(S["oh"], i + 1)
                need(ve, "pos", i - 1)
                tt(chosen[p], oh[:, 0], oh[:, 1], ALU.add).then_inc(S["chosen"], 1)
                ve.wait_ge(S["chosen"], i + 1)
                if i == 0:
                    ve.tensor_copy(total[0], chosen[0]).then_inc(S["total"], 1)
                else:
                    tt(total[p], total[1 - p], chosen[p], ALU.add).then_inc(S["total"], 1)

            def c_slots(i):
                p = i % 2
                ve.wait_ge(S["ed"], i + 1)
                ts(den[:], ed[:], 1.0, None, ALU.add).then_inc(S["den"], 1)
                ve.wait_ge(S["den"], i + 1)
                ve.reciprocal(xl[p][:, D + 2:D + 3], den[:]).then_inc(S["w0"], 1)
                ve.wait_ge(S["w0"], i + 1)
                tt(xl[p][:, D + 3:D + 4], ed[:], xl[p][:, D + 2:D + 3], ALU.mult).then_inc(S["meta"], 1)
                ve.wait_ge(S["pos"], i + 1)
                need(ve, "atu", i)
                for k in range(2):
                    last = ve.tensor_tensor_reduce(junk[:, k], ppos, oh[:, k], 1.0, 0.0, ALU.mult, ALU.add,
                                                   slot[:, k:k + 1])
                last.then_inc(S["slot"], 1)

            ve.memset(epsc[:, 0:1], EPS)
            ve.memset(epsc[:, 1:2], 1e-6)
            for p in range(2):
                ve.memset(logmel[p][32:64], 1.0)
                ve.memset(uT[p][DC:DC + 1], 1.0)
                ve.memset(vT[p][DC:DC + 1], 1.0)
                ve.memset(z[p][:, :, :, 0:KW - 1], 0.0)
            ve.memset(onesb[:], 1.0).then_inc(S["zeroed"], 1)
            ve.memset(fill[:], 0.0).then_inc(S["zeroed"], 1)
            ve.wait_ge(S["zeroed"], 2)
            ve.memset(fill[:, :, D:D + 1], NOWHERE).then_inc(S["zeroed"], 1)

            def h_fil(i):
                ve.wait_ge(S["dec"], 1)
                for k in range(2):
                    last = ts(hdec[:, k], hdec[:, k], winb[:, k:k + 1], None, ALU.add)
                last.then_inc(S["decb"], 1)
                ve.wait_ge(S["decb"], 1)
                tt(hfil[:, 0], hfil[:, 0], hdec[:], ALU.mult)
                tt(hfil[:, 1], hfil[:, 1], hdec[:], ALU.mult).then_inc(S["fil"], 1)

            def h_norm(i):
                ve.wait_ge(S["filT"], 1)
                src = PB[7][0:T, 0:2 * D].rearrange("p (o d) -> p o d", o=2)
                ve.tensor_reduce(habs[:], src, AX.X, ALU.add, apply_absolute_value=True).then_inc(S["habs"], 1)
                ve.wait_ge(S["habs"], 1)
                ve.reciprocal(hrec[:], habs[:]).then_inc(S["hrec"], 1)
                ve.wait_ge(S["hrec"], 1)
                for o in range(2):
                    last = ts(hT[:, o], src[:, o], hrec[:, o:o + 1], None, ALU.mult)
                last.then_inc(S["hT"], 1)
                ve.wait_ge(S["hT"], 1)
                tt(hT[0:1], hT[0:1], bmat[:], ALU.add).then_inc(S["hb"], 1)

            def h_coef(i, o):
                ve.wait_ge(S[f"hc{o}"], 1)
                ve.tensor_copy(hcoef[:, o, 0:2].rearrange("p c d -> p (c d)"), pf01)
                ve.tensor_copy(hcoef[:, o, 2], pf2).then_inc(S[f"hcoef{o}"], 1)

            def h_bf(i):
                ve.wait_ge(S["in_lin"], 16)
                ve.wait_ge(S["in_ffn"], 16)
                ve.tensor_copy(selr[:], sel)
                ve.tensor_copy(causalb[:], causal[:])
                ve.tensor_copy(beforeb[:], before[:])
                ve.tensor_copy(identb[:], ident[:]).then_inc(S["bf"], 1)

            def e_wl(e):
                ve.wait_ge(S["wfch"], e + 1)
                need(ve, "fc", MC * (e - 1))
                tt(wfcl[:, e % 2], wfc[:, e % 2], wfch[:, e % 2].bitcast(F32), ALU.subtract).then_inc(S["wfcl"], 1)
                ve.wait_ge(S["wprh"], e + 1)
                need(ve, "pr", SQ * (e - 1))
                tt(wprl[:, e % 2], wpr[:, e % 2], wprh[:, e % 2].bitcast(F32), ALU.subtract).then_inc(S["wprl"], 1)

            for j in range(NT + LANES - 1):
                t, i, b, c, k, d, w = lanes(j)
                if b == 0: h_coef(b, 0)
                if ok(d): c_vxs(d, 0)
                if ok(d): c_sc(d)
                if ok(k): b_h1(k)
                if ok(d): c_vxs(d, 1)
                if ok(d): c_pn(d)
                if ok(w): c_route(w)
                if ok(c): a_rsum(c)
                if ok(c): b_prod(c, 0)
                if ok(d): c_vxs(d, 2)
                if ok(k): b_xp(k)
                if ok(c): b_v(c, 0)
                if c == 0: h_bf(c)
                if ok(w): c_slots(w)
                if ok(c): b_prod(c, 1)
                if ok(k): c_kx(k)
                if ok(b): a_conv2(b)
                if t == 0: h_fil(t)
                if ok(i): a_stats(i)
                if ok(d): c_h2(d)
                if ok(b): a_conv3(b)
                if ok(c): b_v(c, 1)
                if ok(i): a_u(i)
                if ok(d): c_xl(d)
                if b == 0: h_coef(b, 1)
                if i == 0: h_norm(i)
                if ok(b): a_nmax(b)
                if ok(b): a_v0(b)

            def e_xTl(e):
                need(ve, "fc", MC * e)
                for k in range(2):
                    ve.wait_ge(S["xeTh"], 2 * e + k + 1)
                    last = stt(xeTl[:, k], PB[k][0:DC, 0:CAP], ln2[:, k:k + 1], xeTh[:, k].bitcast(F32),
                               ALU.mult, ALU.subtract)
                last.then_inc(S["xeTl"], 1)

            def e_meta(e):
                x = xe[e % 2]
                ve.wait_ge(S[f"in_slots{e % 2}"], 16 * (e // 2 + 1))
                if e >= 2:
                    ve.wait_ge(S["added"], 16 * SQ * (e - 1))
                ve.tensor_copy(tok[e % 2], x[:, :, D]).then_inc(S["tki"], 1)
                ts(first[:], x[:, :, D + 1], float(e), None, ALU.is_equal).then_inc(S["wfirst"], 1)
                ve.wait_ge(S["wfirst"], e + 1)
                tt(wa[:], first[:], x[:, :, D + 2], ALU.mult)
                stt(wb[:], first[:], 0.0, x[:, :, D + 3], ALU.is_equal, ALU.mult).then_inc(S["wab"], 1)
                ve.wait_ge(S["wab"], e + 1)
                tt(wt[e % 2], wa[:], wb[:], ALU.add).then_inc(S["wt"], 1)

            e_wl(0)
            e_xTl(0)
            e_meta(0)
            for e in range(E):
                if e < E - 1: e_wl(e + 1)
                for m in range(MC):
                    n = e * MC + m
                    ve.wait_ge(S["gelu"], n + 1)
                    if m == 0:
                        need(ve, "pr", SQ * e)
                    tt(hidl[:, m], gelu[n % 2], hidh[:, m].bitcast(F32), ALU.subtract).then_inc(S["hidl"], 1)
                if e + 1 < E:
                    e_xTl(e + 1)
                    e_meta(e + 1)
                ve.wait_ge(S["wt"], e + 1)
                if e >= 2:
                    ve.wait_ge(S["added"], 16 * SQ * (e - 1))
                for q in range(SQ):
                    ve.wait_ge(S["pr"], SQ * e + q // 2 * 2 + 2)
                    ts(ye[e % 2][:, q], PB[6 + q // 2][0:SR, (q % 2) * D:(q % 2 + 1) * D], wt[e % 2][:, q:q + 1],
                       None, ALU.mult).then_inc(S["ye"], 1)

        @block.gpsimd
        def _(pool):
            def b_hv(i):
                pool.wait_ge(S["v2"], i + 1)
                pool.wait_ge(S["h0"], i + 1)
                need(pool, "h1", i)
                pool.tensor_tensor(hv[:], v[i % 2], h0[i % 3], ALU.add).then_inc(S["hv"], 1)

            def c_vtl(i):
                pool.wait_ge(S["vtr"], i + 1)
                pool.tensor_tensor(vtl[:], vtr[:], vth[:].bitcast(F32), ALU.subtract).then_inc(S["vtl"], 1)

            def c_base(i):
                pool.wait_ge(S["h2"], i + 1)
                pool.wait_ge(S["h1"], i + 1)
                if i >= 2:
                    pool.wait_ge(S[f"stored{i % 2}"], 16 * (i // 2))
                pool.tensor_tensor(base[i % 2], h2[i % 2], h1[i % 2], ALU.add).then_inc(S["base"], 1)

            def c_pnorm(i):
                pool.wait_ge(S["prc"], i + 1)
                need(pool, "pT", i)
                pool.tensor_tensor(pn[:], es[:], prc[:, :, None].broadcast_to([R, HEADS, T]), ALU.mult)\
                    .then_inc(S["pn"], 1)

            def c_index(i):
                p = i % 2
                pool.wait_ge(S["ef"], i + 1)
                pool.wait_ge(S["xl"], i + 1)
                pool.tensor_copy(xl[p][:, D + 1:D + 2], ef[p][:, 0:1])
                pool.tensor_copy(xl[p][:, D:D + 1], token[:, i:i + 1])
                pool.tensor_scalar(row0[:], ef[p], float(CAP), None, ALU.mult).then_inc(S["row0"], 1)
                pool.wait_ge(S["slot"], i + 1)
                pool.tensor_scalar(over[:], slot[:], float(CAP), NOWHERE, ALU.is_ge, ALU.mult).then_inc(S["over"], 1)
                pool.wait_ge(S["row0"], i + 1)
                pool.tensor_tensor(at[:], row0[:], slot[:], ALU.add).then_inc(S["at"], 1)
                pool.wait_ge(S["over"], i + 1)
                pool.wait_ge(S["at"], i + 1)
                pool.tensor_tensor(atf[:], at[:], over[:], ALU.add).then_inc(S["atf"], 1)
                pool.wait_ge(S["atf"], i + 1)
                pool.tensor_copy(atu[p], atf[:]).then_inc(S["atu"], 1)

            def c_scatter(i):
                rows = R if i < NT - 1 else LAST
                if i == 0:
                    pool.wait_ge(S["filled"], 16 * E)
                pool.wait_ge(S["meta"], i + 1)
                pool.wait_ge(S["atu"], i + 1)
                for k in range(TOPK):
                    pool.indirect_dma_start(
                        slots, bass.IndirectOffsetOnAxis(ap=atu[i % 2][0:rows, k:k + 1], axis=0),
                        xl[i % 2][0:rows, :], None, bounds_check=E * CAP - 1, oob_is_err=False)\
                        .then_inc(S[f"scattered{i % 2}"], 16)

            for j in range(NT + LANES - 1):
                t, i, b, c, k, d, w = lanes(j)
                if ok(d): c_pnorm(d)
                if ok(k): c_vtl(k)
                if ok(w): c_index(w)
                if ok(w): c_scatter(w)
                if ok(d): c_base(d)
                if ok(c): b_hv(c)

            for p in range(2):
                pool.wait_ge(S[f"stored{p}"], 16 * ((NT + 1 - p) // 2))
            for e in range(E):
                if e:
                    pool.wait_ge(S["added"], 16 * SQ * e)
                for q in range(SQ):
                    pool.wait_ge(S["ye"], SQ * e + q + 1)
                    pool.indirect_dma_start(
                        out, bass.IndirectOffsetOnAxis(ap=tok[e % 2][:, q:q + 1], axis=0),
                        ye[e % 2][:, q], None, bounds_check=TOKENS - 1, oob_is_err=False,
                        compute_op=ALU.add).then_inc(S["added"], 16)


def layout(x, i):
    import numpy as np
    d = {k: np.asarray(w) for k, w in i.items()}
    x = np.asarray(x)
    o = {}
    order = np.minimum(np.arange(NT * G), B - 1)
    fr = np.stack([x[:, n * HOP:n * HOP + FRAME] for n in range(T)], 1)[order]
    o["frames"] = fr.reshape(NT * R, FRAME).T
    mel = d["L0_tok_mel_filters"].T
    o["melT"] = np.concatenate([mel, mel], 0)
    o["dct"] = d["L0_tok_dct"]
    o["w_proj"] = d["L0_tok_w_proj"]
    b = d["L0_tok_b_proj"][None]
    o["tokw"] = np.concatenate([np.zeros((MELS, D), b.dtype), b], 0)

    def chunks(w, extra=None):
        w = w.reshape(2, DC, -1).transpose(1, 0, 2)
        if extra is not None:
            w = np.concatenate([w, np.broadcast_to(extra, (1, 2, w.shape[2]))], 0)
        return w

    o["wlin"] = chunks(d["L0_attn_W_lin"].T, d["L0_attn_b_lin"])
    pad = lambda w: np.concatenate([w, np.zeros((5 * 128 - 3 * D,) + w.shape[1:], w.dtype)], 0)
    o["taps"] = pad(d["L0_attn_conv_w"][:, 0]).reshape(5, 128, KW).transpose(1, 0, 2)
    o["tapb"] = pad(d["L0_attn_conv_b"]).reshape(5, 128).T
    o["hfil"] = d["L0_attn_h_param"][:, :, :T].reshape(2, 2, DC, T).transpose(2, 0, 1, 3)
    o["alph"] = d["L0_attn_alphas"].reshape(2, DC).T
    o["winb"] = d["L0_attn_win_b"].reshape(2, DC).T
    o["bmat"] = d["L0_attn_Bmat"].reshape(1, 2, D)
    o["wout"] = chunks(d["L0_attn_W_out"].T, d["L0_attn_b_out"])
    o["ln1"] = d["L0_ffn_ln1_w"].reshape(2, DC).T
    o["ln2"] = d["L0_ffn_ln2_w"].reshape(2, DC).T
    o["wqkv"] = chunks(d["L0_ffn_c_attn_w"].T)
    w = d["L0_ffn_c_proj_w"].T
    o["wo"] = np.concatenate([w, np.zeros((64, D), w.dtype)], 0).reshape(2, 128, D).transpose(1, 0, 2)
    o["wgate"] = chunks(d["L0_ffn_w_g"].T)
    o["c_fc"] = d["L0_ffn_c_fc"]
    o["c_proj_e"] = d["L0_ffn_c_proj_e"]
    return o


def packs(o):
    import numpy as np
    for group, items in PACKS.items():
        cols = []
        for name, rows, *dims in items:
            w = np.zeros((128, size(dims)), np.float32)
            w[:rows] = np.asarray(o.pop(name)).reshape(rows, -1)
            cols.append(w)
        o[group] = np.concatenate(cols, 1)
    return o


def kernel(x, **inputs):
    import numpy as np
    import concourse.bacc as bacc
    from concourse.bass_utils import run_bass_kernel_spmd

    nc = bacc.Bacc("TRN2", target_bir_lowering=False, num_devices=1)
    arrays, a = {}, {}
    for name, value in packs({**layout(x, inputs), **constants()}).items():
        value = np.ascontiguousarray(value)
        arrays["in_" + name] = value
        a[name] = nc.dram_tensor("in_" + name, value.shape, mybir.dt.from_np(value.dtype), kind="ExternalInput").ap()
    out = nc.dram_tensor("out_0", (TOKENS, D), F32, kind="ExternalOutput").ap()
    tower(nc, a, out)
    r = run_bass_kernel_spmd(nc, [arrays], core_ids=[0])
    return r.results[0]["out_0"].reshape(B, T, D)
```
